# Optimizing a Trainium2 kernel written in Bass

```python
import numpy as np
import jax
import jax.numpy as jnp

def _softmax(x, axis=-1):
    return jax.nn.softmax(x, axis=axis)

def _gelu(x):
    return jax.nn.gelu(x, approximate=True)

def _silu(x):
    return jax.nn.silu(x)

def _sigmoid(x):
    return jax.nn.sigmoid(x)

def _layernorm(x, axis=-1, eps=1e-05):
    m = jnp.mean(x, axis=axis, keepdims=True)
    v = jnp.var(x, axis=axis, keepdims=True)
    return (x - m) / jnp.sqrt(v + eps)

def _scatter_add(tgt, idx, src, axis=0):
    return tgt.at[idx].add(src)

def _segment_sum(src, seg, n):
    return jax.ops.segment_sum(src, seg, n)
kernel_name = 'mk_macaron_d1_jaxref_r8_d9d753'

def setup_inputs(seed: int=0):
    np.random.seed(seed)
    _w = jnp.asarray

    def _L0_attn_setup():
        import jax, jax.numpy as jnp
        import numpy as np
        B, S, D_IN, D_OUT, H = (2, 256, 128, 128, 16)
        HD = D_OUT // H
        key = jax.random.key(seed)
        ks = jax.random.split(key, 6)
        scale = 0.02
        return {'x': jax.random.normal(ks[0], (B, S, D_IN), dtype=jnp.float32), 'Wq': jax.random.normal(ks[1], (D_IN, D_OUT), dtype=jnp.float32) * scale, 'Wk': jax.random.normal(ks[2], (D_IN, D_OUT), dtype=jnp.float32) * scale, 'Wv': jax.random.normal(ks[3], (D_IN, D_OUT), dtype=jnp.float32) * scale, 'Wo': jax.random.normal(ks[4], (D_OUT, D_OUT), dtype=jnp.float32) * scale, 'bo': jax.random.normal(ks[5], (D_OUT,), dtype=jnp.float32) * scale}
    _L0_attn_in = _L0_attn_setup()

    def _L0_ffn_setup():
        import jax, jax.numpy as jnp
        import numpy as np
        import math
        B, T, D, H, E, TOPK, CAPF = (4, 256, 128, 16, 8, 2, 2.0)
        HD = D // H

        def layernorm(x, g, b, eps=1e-05):
            m = jnp.mean(x, -1, keepdims=True)
            v = jnp.mean(jnp.square(x - m), -1, keepdims=True)
            return (x - m) * jax.lax.rsqrt(v + eps) * g + b

        def block_forward(x, ln1_g, ln1_b, Wqkv, Wproj, ln2_g, ln2_b, Wgate, W1, b1, W2, b2):
            Bb, Tt, d = x.shape
            hd = HD
            half = hd // 2
            h = layernorm(x, ln1_g, ln1_b)
            qkv = (h @ Wqkv).reshape(Bb, Tt, H, 3 * hd)
            q, k, v = (qkv[..., :hd], qkv[..., hd:2 * hd], qkv[..., 2 * hd:])
            inv_freq = 1.0 / 10000.0 ** (jnp.arange(0, hd, 2, dtype=jnp.float32) / hd)
            ang = jnp.arange(Tt, dtype=jnp.float32)[:, None] * inv_freq
            sin = jnp.sin(ang)[None, :, None, :].astype(x.dtype)
            cos = jnp.cos(ang)[None, :, None, :].astype(x.dtype)

            def rope(t):
                t1, t2 = (t[..., :half], t[..., half:])
                return jnp.concatenate([t1 * cos - t2 * sin, t1 * sin + t2 * cos], -1)
            q, k = (rope(q), rope(k))
            scores = jnp.einsum('bqhd,bkhd->bhqk', q, k) / math.sqrt(hd)
            causal = jnp.tril(jnp.ones((Tt, Tt), dtype=bool))
            scores = jnp.where(causal, scores, jnp.asarray(-1000000000.0, scores.dtype))
            probs = jax.nn.softmax(scores, axis=-1)
            attn = jnp.einsum('bhqk,bkhd->bqhd', probs, v).reshape(Bb, Tt, d) @ Wproj
            x = x + attn
            h2 = layernorm(x, ln2_g, ln2_b)
            flat = h2.reshape(-1, d)
            N = flat.shape[0]
            capacity = int(math.ceil(CAPF * N / E))
            gates = jax.nn.softmax((flat @ Wgate).astype(jnp.float32), -1).astype(flat.dtype)
            _, top_inds = jax.lax.top_k(gates, TOPK)
            mask = jnp.zeros((N, E), dtype=bool).at[jnp.arange(N)[:, None], top_inds].set(True)
            pos = jnp.cumsum(mask.astype(jnp.int32), axis=0) * mask - 1
            keep = (pos < capacity) & mask
            t_flat = jnp.repeat(jnp.arange(N), TOPK)
            e_flat = top_inds.reshape(-1)
            p = pos[t_flat, e_flat]
            kp = keep[t_flat, e_flat]
            p_eff = jnp.where(kp, p, capacity)
            exp_in = jnp.zeros((E, capacity, d), flat.dtype).at[e_flat, p_eff].set(flat[t_flat], mode='drop')
            hmid = jax.nn.gelu(jnp.einsum('ecd,edf->ecf', exp_in, W1) + b1[:, None, :], approximate=False)
            exp_out = jnp.einsum('ecf,efd->ecd', hmid, W2) + b2[:, None, :]
            gate = gates[t_flat, e_flat] * kp.astype(flat.dtype)
            p_g = jnp.minimum(p_eff, capacity - 1)
            moe = jnp.zeros((N, d), flat.dtype).at[t_flat].add(exp_out[e_flat, p_g] * gate[:, None])
            return x + moe.reshape(Bb, Tt, d)
        key = jax.random.key(seed)
        ks = jax.random.split(key, 8)
        s = 0.02
        return {'x': jax.random.normal(ks[0], (B, T, D), jnp.float32), 'ln1_g': jnp.ones((D,), jnp.float32), 'ln1_b': jnp.zeros((D,), jnp.float32), 'Wqkv': jax.random.normal(ks[1], (D, 3 * D), jnp.float32) * s, 'Wproj': jax.random.normal(ks[2], (D, D), jnp.float32) * s, 'ln2_g': jnp.ones((D,), jnp.float32), 'ln2_b': jnp.zeros((D,), jnp.float32), 'Wgate': jax.random.normal(ks[3], (D, E), jnp.float32) * s, 'W1': jax.random.normal(ks[4], (E, D, 4 * D), jnp.float32) * s, 'b1': jnp.zeros((E, 4 * D), jnp.float32), 'W2': jax.random.normal(ks[5], (E, 4 * D, D), jnp.float32) * s, 'b2': jnp.zeros((E, D), jnp.float32)}
    _L0_ffn_in = _L0_ffn_setup()
    _d = {'L0_attn_x': _L0_attn_in['x'], 'L0_attn_Wq': _L0_attn_in['Wq'], 'L0_attn_Wk': _L0_attn_in['Wk'], 'L0_attn_Wv': _L0_attn_in['Wv'], 'L0_attn_Wo': _L0_attn_in['Wo'], 'L0_attn_bo': _L0_attn_in['bo'], 'L0_ffn_ln1_g': _L0_ffn_in['ln1_g'], 'L0_ffn_ln1_b': _L0_ffn_in['ln1_b'], 'L0_ffn_Wqkv': _L0_ffn_in['Wqkv'], 'L0_ffn_Wproj': _L0_ffn_in['Wproj'], 'L0_ffn_ln2_g': _L0_ffn_in['ln2_g'], 'L0_ffn_ln2_b': _L0_ffn_in['ln2_b'], 'L0_ffn_Wgate': _L0_ffn_in['Wgate'], 'L0_ffn_W1': _L0_ffn_in['W1'], 'L0_ffn_b1': _L0_ffn_in['b1'], 'L0_ffn_W2': _L0_ffn_in['W2'], 'L0_ffn_b2': _L0_ffn_in['b2']}
    _x0 = _d['L0_attn_x']
    _d['L0_attn_x'] = jax.random.normal(jax.random.fold_in(jax.random.key(seed), 1), (32, 256, 128), dtype=_x0.dtype)
    del _x0
    return _d

def reference(L0_attn_x, L0_attn_Wq, L0_attn_Wk, L0_attn_Wv, L0_attn_Wo, L0_attn_bo, L0_ffn_ln1_g, L0_ffn_ln1_b, L0_ffn_Wqkv, L0_ffn_Wproj, L0_ffn_ln2_g, L0_ffn_ln2_b, L0_ffn_Wgate, L0_ffn_W1, L0_ffn_b1, L0_ffn_W2, L0_ffn_b2):

    def _L0_attn_ref(x, Wq, Wk, Wv, Wo, bo):
        import jax, jax.numpy as jnp
        import numpy as np
        B, S, D_IN, D_OUT, H = (2, 256, 128, 128, 16)
        HD = D_OUT // H
        b, s, _ = x.shape
        q = (x @ Wq).reshape(b, s, H, HD).transpose(0, 2, 1, 3)
        k = (x @ Wk).reshape(b, s, H, HD).transpose(0, 2, 1, 3)
        v = (x @ Wv).reshape(b, s, H, HD).transpose(0, 2, 1, 3)
        scores = jnp.einsum('bhqd,bhkd->bhqk', q, k) / jnp.sqrt(jnp.float32(HD))
        causal = jnp.tril(jnp.ones((s, s), dtype=bool))
        scores = jnp.where(causal[None, None], scores, -jnp.inf)
        attn = jax.nn.softmax(scores, axis=-1)
        out = jnp.einsum('bhqk,bhkd->bhqd', attn, v)
        out = out.transpose(0, 2, 1, 3).reshape(b, s, D_OUT)
        return out @ Wo + bo

    def _L0_ffn_ref(x, ln1_g, ln1_b, Wqkv, Wproj, ln2_g, ln2_b, Wgate, W1, b1, W2, b2):
        import jax, jax.numpy as jnp
        import numpy as np
        import math
        B, T, D, H, E, TOPK, CAPF = (4, 256, 128, 16, 8, 2, 2.0)
        HD = D // H

        def layernorm(x, g, b, eps=1e-05):
            m = jnp.mean(x, -1, keepdims=True)
            v = jnp.mean(jnp.square(x - m), -1, keepdims=True)
            return (x - m) * jax.lax.rsqrt(v + eps) * g + b

        def block_forward(x, ln1_g, ln1_b, Wqkv, Wproj, ln2_g, ln2_b, Wgate, W1, b1, W2, b2):
            Bb, Tt, d = x.shape
            hd = HD
            half = hd // 2
            h = layernorm(x, ln1_g, ln1_b)
            qkv = (h @ Wqkv).reshape(Bb, Tt, H, 3 * hd)
            q, k, v = (qkv[..., :hd], qkv[..., hd:2 * hd], qkv[..., 2 * hd:])
            inv_freq = 1.0 / 10000.0 ** (jnp.arange(0, hd, 2, dtype=jnp.float32) / hd)
            ang = jnp.arange(Tt, dtype=jnp.float32)[:, None] * inv_freq
            sin = jnp.sin(ang)[None, :, None, :].astype(x.dtype)
            cos = jnp.cos(ang)[None, :, None, :].astype(x.dtype)

            def rope(t):
                t1, t2 = (t[..., :half], t[..., half:])
                return jnp.concatenate([t1 * cos - t2 * sin, t1 * sin + t2 * cos], -1)
            q, k = (rope(q), rope(k))
            scores = jnp.einsum('bqhd,bkhd->bhqk', q, k) / math.sqrt(hd)
            causal = jnp.tril(jnp.ones((Tt, Tt), dtype=bool))
            scores = jnp.where(causal, scores, jnp.asarray(-1000000000.0, scores.dtype))
            probs = jax.nn.softmax(scores, axis=-1)
            attn = jnp.einsum('bhqk,bkhd->bqhd', probs, v).reshape(Bb, Tt, d) @ Wproj
            x = x + attn
            h2 = layernorm(x, ln2_g, ln2_b)
            flat = h2.reshape(-1, d)
            N = flat.shape[0]
            capacity = int(math.ceil(CAPF * N / E))
            gates = jax.nn.softmax((flat @ Wgate).astype(jnp.float32), -1).astype(flat.dtype)
            _, top_inds = jax.lax.top_k(gates, TOPK)
            mask = jnp.zeros((N, E), dtype=bool).at[jnp.arange(N)[:, None], top_inds].set(True)
            pos = jnp.cumsum(mask.astype(jnp.int32), axis=0) * mask - 1
            keep = (pos < capacity) & mask
            t_flat = jnp.repeat(jnp.arange(N), TOPK)
            e_flat = top_inds.reshape(-1)
            p = pos[t_flat, e_flat]
            kp = keep[t_flat, e_flat]
            p_eff = jnp.where(kp, p, capacity)
            exp_in = jnp.zeros((E, capacity, d), flat.dtype).at[e_flat, p_eff].set(flat[t_flat], mode='drop')
            hmid = jax.nn.gelu(jnp.einsum('ecd,edf->ecf', exp_in, W1) + b1[:, None, :], approximate=False)
            exp_out = jnp.einsum('ecf,efd->ecd', hmid, W2) + b2[:, None, :]
            gate = gates[t_flat, e_flat] * kp.astype(flat.dtype)
            p_g = jnp.minimum(p_eff, capacity - 1)
            moe = jnp.zeros((N, d), flat.dtype).at[t_flat].add(exp_out[e_flat, p_g] * gate[:, None])
            return x + moe.reshape(Bb, Tt, d)
        return block_forward(x, ln1_g, ln1_b, Wqkv, Wproj, ln2_g, ln2_b, Wgate, W1, b1, W2, b2)
    x = L0_attn_x
    x = x + 0.5 * _L0_ffn_ref(_layernorm(x, axis=-1), L0_ffn_ln1_g, L0_ffn_ln1_b, L0_ffn_Wqkv, L0_ffn_Wproj, L0_ffn_ln2_g, L0_ffn_ln2_b, L0_ffn_Wgate, L0_ffn_W1, L0_ffn_b1, L0_ffn_W2, L0_ffn_b2)
    x = x + _L0_attn_ref(_layernorm(x, axis=-1), L0_attn_Wq, L0_attn_Wk, L0_attn_Wv, L0_attn_Wo, L0_attn_bo)
    x = x + 0.5 * _L0_ffn_ref(_layernorm(x, axis=-1), L0_ffn_ln1_g, L0_ffn_ln1_b, L0_ffn_Wqkv, L0_ffn_Wproj, L0_ffn_ln2_g, L0_ffn_ln2_b, L0_ffn_Wgate, L0_ffn_W1, L0_ffn_b1, L0_ffn_W2, L0_ffn_b2)
    return x

_drawn_inputs = setup_inputs


def setup_inputs(seed=0):
    import zlib

    import numpy as np

    out = dict(_drawn_inputs(seed))
    spreads = {'L0_ffn_ln1_g': (1.0, 0.6),
     'L0_ffn_ln1_b': (0.0, 0.8),
     'L0_ffn_ln2_g': (1.0, 0.6),
     'L0_ffn_ln2_b': (0.0, 0.8),
     'L0_ffn_b1': (0.0, 0.8),
     'L0_ffn_b2': (0.0, 0.632)}
    factors = {'L0_attn_Wq': 8.0,
     'L0_attn_Wk': 8.0,
     'L0_attn_Wv': 8.0,
     'L0_attn_Wo': 8.0,
     'L0_attn_bo': 3.612,
     'L0_ffn_Wqkv': 8.0,
     'L0_ffn_Wproj': 8.0,
     'L0_ffn_Wgate': 4.389,
     'L0_ffn_W1': 7.902,
     'L0_ffn_W2': 7.174}
    for name, (base, spread) in spreads.items():
        noise = np.random.default_rng([zlib.crc32(name.encode()), seed]).standard_normal(out[name].shape)
        drawn = base * np.exp(spread * noise) if base else spread * noise
        out[name] = jnp.asarray(drawn.astype(out[name].dtype))
    for name, factor in factors.items():
        out[name] = (out[name] * factor).astype(out[name].dtype)
    return out
```

```python
from contextlib import ExitStack

import numpy as np

import concourse.bass as bass
from concourse import mybir

F32 = mybir.dt.float32
BF16 = mybir.dt.bfloat16
I32 = mybir.dt.int32
U32 = mybir.dt.uint32
ALU = mybir.AluOpType
ACT = mybir.ActivationFunctionType
AX = mybir.AxisListType

P = 128
D = 128
H = 16
HD = D // H
NB = 32
T = 2
S = T * P
N = NB * S
E = 8
TOPK = 2
CAP = (2 * N + E - 1) // E
F = 4 * D
FC = F // P
GROUP = 4 * P
EPS = 1e-5
SCALE = float(HD) ** -0.5
BIG = 1e30
JP = H // 2
NQK = 7 * HD
NMAX = 3
DROP = float(1 << 20)

RING = 3
RING_ORDER = {
    "ffn": [("S0", 1), ("ST0", 0), ("S1", 1), ("ST1", 0), ("S2", 1), ("ST2", 0), ("S3", 1),
            ("ST3", 0), ("PR", -1), ("S4", 1), ("ST4", 0), ("S5", 1), ("ST5", 0), ("QT", 2), ("KT", 2),
            ("Z2", -1), ("MT", 1), ("QKV", 3), ("CM", -2), ("LG", -1), ("OT", 0)],
    "plain": [("S0", 1), ("ST0", 0), ("S1", 1), ("ST1", 0), ("S2", 1), ("ST2", 0), ("S3", 1),
              ("ST3", 0), ("PR", -1), ("S4", 1), ("ST4", 0), ("S5", 1), ("ST5", 0), ("QT", 2),
              ("KT", 2), ("MT", 1), ("QKV", 3), ("OT", 0)],
}
FIRST, LAST = -5, NB + 1
STEADY = (4, NB - 6)

S_UNITS = [(0, 0, 4), (1, 0, 2), (1, 2, 2), (0, 4, 4), (1, 4, 2), (1, 6, 2)]
ST_UNITS = [(0, 0, 2), (0, 2, 2), (1, 0, 4), (0, 4, 2), (0, 6, 2), (1, 4, 4)]


class Seq:

    def __init__(self, reg, const):
        self.reg, self.const, self.par = reg, const, const % 2

    def __add__(self, k):
        return Seq(self.reg, self.const + k)

    def live(self):
        return self.reg is not None or 0 <= self.const < NB

    def count(self, per, extra=0):
        fixed = per * self.const + extra
        return fixed if self.reg is None else self.reg * (2 * per) + fixed

    def of_parity(self, per):
        fixed = per * ((self.const - self.par) // 2 + 1)
        return fixed if self.reg is None else self.reg * per + fixed


def some(value):
    return not isinstance(value, int) or value > 0


def computed(eng, value):
    if not isinstance(value, int):
        eng.compute_val(value)
    return value


def iterations(eng, body):
    for b in range(FIRST, STEADY[0]):
        body(Seq(None, b))
    with eng.Fori(STEADY[0] // 2, STEADY[1] // 2) as i:
        body(Seq(i, 0))
        body(Seq(i, 1))
    for b in range(STEADY[1], LAST + 1):
        body(Seq(None, b))


def new_semaphore(nc, sems, name):
    sems.append(nc.alloc_semaphore(name=name))
    return sems[-1]


def give_back(nc, sems):
    nc.clear_and_free_semaphores(sems)
    nc.all_engine_barrier()


class Ring:

    def __init__(self, kind):
        self.at, n = {}, 0
        self.per = len(RING_ORDER[kind])
        assert self.per % RING == 0
        for b in range(FIRST, LAST + 1):
            for name, ahead in RING_ORDER[kind]:
                if 0 <= b + ahead < NB:
                    self.at[name, b + ahead] = n
                    n += 1

    def use(self, name, c):
        ref = c.const if c.reg is None else 8 + c.const
        n = self.at[name, ref]
        fixed = n // RING
        if c.reg is None:
            return n % RING, fixed
        k = self.per // RING
        return n % RING, c.reg * (2 * k) + (fixed - 8 * k)


def attention_pass(nc, kind, r):
    ffn = kind == "ffn"
    ring = Ring(kind)
    sems = []
    with ExitStack() as ctx:
        def sb(name, shape, dt=F32):
            return ctx.enter_context(nc.sbuf_tensor(f"{name}_{r.tag}", shape, dt))

        def sem(name):
            return new_semaphore(nc, sems, f"{name}_{r.tag}")

        psum = ctx.enter_context(nc.psum_tensor(f"psum_{r.tag}", [P, 8, 512], F32))
        o_bank = psum[:, 6, :]
        zt_ps = psum[:, 7, 0:S]
        at_ps = psum[:, 7, S:2 * S]

        def slot(n):
            return psum[:, 2 * n:2 * n + 2, :]

        z = sb("z", [P, 2, T, D])
        hT = sb("hT", [P, S])
        qk = sb("qk", [P, 2, T * H, HD])
        vraw = sb("vraw", [P, 2, T, D])
        residual = sb("residual", [P, 2, T * H, HD])
        stack = sb("stack", [P, 2, 2, T * H, 8, HD], BF16)
        QT = sb("QT", [P, 2, JP, S], BF16)
        KT = sb("KT", [P, 2, JP, S], BF16)
        mparts = sb("mparts", [P, T, 2, NMAX, JP], BF16)
        mT = sb("mT", [2 * NMAX * JP, S], BF16)
        nmax = sb("nmax", [P, T * H])
        nmax_rest = sb("nmax_rest", [P, T * H])
        V = sb("V", [P, 2, T, H, 32])
        probs0 = sb("probs0", [P, H, S])
        probs1 = sb("probs1", [P, H, P])
        OT = sb("OT", [P, 4, S])
        rden = sb("rden", [P, T, H])
        attn = sb("attn", [P, T, H, HD])
        attnT = sb("attnT", [P, S])
        stats = sb("stats", [P, 3, T, 6])
        mv = sb("mv", [P, 3, T, 2])
        var_eps = sb("var_eps", [P, 3, T])
        rstd = sb("rstd", [P, 3, T])
        again = sb("again", [P, T])
        wqkv = sb("wqkv", [D, 3 * D])
        wout = sb("wout", [D, D])
        if ffn:
            cos = sb("cos", [P, T, HD])
            sin = sb("sin", [P, T, HD])
            swapped = sb("swapped", [P, T, 2 * H, HD])
            g1 = sb("g1", [D, 1])
            b1 = sb("b1", [D, 1])
            g2 = sb("g2", [D, 1])
            b2 = sb("b2", [D, 1])
            wgate = sb("wgate", [D, E])
            z2 = sb("z2", [P, 2, T, D])
            h2T = sb("h2T", [P, S])
            nlmax = sb("nlmax", [P, T])
            lshift = sb("lshift", [P, T, E])
            gexp = sb("gexp", [P, T, E])
            gsum = sb("gsum", [P, T])
            gates = sb("gates", [P, T, E])
            top = sb("top", [P, T, 8])
            top_at = sb("top_at", [P, T, 8], U32)
            expert = sb("expert", [P, T, TOPK])
            onehot = sb("onehot", [P, T, TOPK, E])
            chosen = sb("chosen", [P, T, E], BF16)
            carry = sb("carry", [P, E])
            count = sb("count", [P, T, E])
            picked = sb("picked", [P, T, TOPK, E])
            pos = sb("pos", [P, T * TOPK])
            over = sb("over", [P, T * TOPK])
            place = sb("place", [P, T * TOPK])
            send_f = sb("send_f", [P, T * TOPK])
            send_to = sb("send_to", [P, 2, T * TOPK], I32)
        else:
            bias = sb("bias", [P, D])
            eo = sb("eo", [P, 2, T * TOPK, D])
            read_at = sb("read_at", [P, 2, T * TOPK], I32)
            moe = sb("moe", [P, T, D])

        loaded = sem("loaded")
        consts_ready = sem("consts_ready")
        begun = sem("begun")
        sp_begun = sem("sp_begun")
        x_loaded = [sem(f"x_loaded{n}") for n in range(2)]
        drained = [sem(f"drained{n}") for n in range(RING)]
        filled = [sem(f"filled{n}") for n in range(RING)]
        var_ready = [sem(f"var_ready{n}") for n in range(3)]
        rstd_ready = [sem(f"rstd_ready{n}") for n in range(3)]
        z_ready = sem("z_ready")
        zt_done = sem("zt_done")
        hT_ready = sem("hT_ready")
        qk_copied = sem("qk_copied")
        rotated = sem("rotated")
        part1_ready = sem("part1_ready")
        rest_ready = sem("rest_ready")
        part2_ready = sem("part2_ready")
        part3_ready = sem("part3_ready")
        QT_ready = sem("QT_ready")
        KT_ready = sem("KT_ready")
        m_ready = sem("m_ready")
        mT_ready = sem("mT_ready")
        max_rows_in = sem("max_rows_in")
        probs_ready = sem("probs_ready")
        V_ready = sem("V_ready")
        pv_done = sem("pv_done")
        OT_ready = sem("OT_ready")
        attn_ready = sem("attn_ready")
        at_done = sem("at_done")
        attnT_ready = sem("attnT_ready")
        if ffn:
            z2_ready = sem("z2_ready")
            h2T_ready = sem("h2T_ready")
            shift_ready = sem("shift_ready")
            gexp_ready = sem("gexp_ready")
            chosen_ready = sem("chosen_ready")
            send_ready = sem("send_ready")
            sent = [sem(f"sent{n}") for n in range(2)]
        else:
            gathered = [sem(f"gathered{n}") for n in range(2)]
            combined = sem("combined")
            index_ready = sem("index_ready")

        block = ctx.enter_context(nc.Block())

        rows = [slice(64 * a, 64 * a + NQK) for a in range(2)]
        rows_m = [slice(64 * a, 64 * a + NQK + NMAX) for a in range(2)]

        @block.sync
        def _(sp):
            sp.sem_inc(sp_begun, 1)
            loads = [(wqkv[:], r.wqkv), (wout[:], r.wout)]
            if ffn:
                loads += [(g1[:], r.ln1_g), (b1[:], r.ln1_b), (g2[:], r.ln2_g), (b2[:], r.ln2_b),
                          (wgate[:], r.wgate), (cos[:], r.cos), (sin[:], r.sin)]
            else:
                loads += [(bias[:], r.bias.to_broadcast([P, D]))]
            for dst, src in loads:
                sp.dma_start(dst, src).then_inc(loaded, 16)

            def load(c):
                if some(due := computed(sp, (c + -2).of_parity(16))):
                    sp.wait_ge(sp_begun, 1)
                    sp.wait_ge(x_loaded[c.par], due)
                sp.dma_start(r.X[:, bass.ds(c.count(S), S)].rearrange("p (t d) -> p t d", t=T),
                             r.x[bass.ds(c.count(S), S), :].rearrange("(t p) d -> p t d", p=P)
                             ).then_inc(x_loaded[c.par], 16)

            def place_max_rows(c):
                due = computed(sp, c.count(1, 1))
                sp.wait_ge(sp_begun, 1)
                sp.wait_ge(mT_ready, due)
                for a in range(2):
                    for k in range(NMAX):
                        row, at = 64 * a + NQK + k, (a * NMAX + k) * JP
                        sp.dma_start(QT[row:row + 1, c.par, :, :],
                                     mT[at:at + JP, :]).then_inc(max_rows_in, 16)

            def body(b):
                if r.loads_x and (b + 6).live():
                    load(b + 6)
                if (b + 1).live():
                    place_max_rows(b + 1)

            if r.loads_x:
                load(Seq(None, 0))
            iterations(sp, body)
            sp.wait_ge(loaded, 16 * len(loads))
        n_loads = 9 if ffn else 3

        @block.tensor
        def _(pe):
            pe.wait_ge(loaded, 16 * n_loads)
            pe.wait_ge(consts_ready, 3 if ffn else 2)

            def transposed_values(c):
                pe.wait_ge(OT_ready, c.count(2, 2))
                n, uses = ring.use("OT", c)
                if some(uses):
                    pe.wait_ge(drained[n], uses)
                for t in range(T):
                    for s in range(4):
                        last = nc.tensor.transpose(slot(n)[:, t, s * P:(s + 1) * P],
                                                   OT[:, s, t * P:(t + 1) * P], r.identf[:])
                last.then_inc(filled[n], 1)

            def transpose_z(c):
                pe.wait_ge(z_ready, c.count(1, 1))
                if some(due := c.count(1)):
                    pe.wait_ge(hT_ready, due)
                for t in range(T):
                    last = nc.tensor.transpose(zt_ps[:, t * P:(t + 1) * P], z[:, c.par, t, :], r.identf[:])
                last.then_inc(zt_done, 1)

            def qkv(c):
                pe.wait_ge(hT_ready, c.count(1, 1))
                n, uses = ring.use("QKV", c)
                if some(uses):
                    pe.wait_ge(drained[n], uses)
                for t in range(T):
                    last = nc.tensor.matmul(slot(n)[:, t, 0:3 * D], hT[:, t * P:(t + 1) * P], wqkv[:],
                                            start=True, stop=True)
                last.then_inc(filled[n], 1)

            def maxima_unit(u, c):
                t, j0, nj = S_UNITS[u]
                if u == 0:
                    pe.wait_ge(QT_ready, c.count(1, 1))
                    pe.wait_ge(KT_ready, c.count(1, 1))
                n, uses = ring.use(f"S{u}", c)
                if some(uses):
                    pe.wait_ge(drained[n], uses)
                for a in range(2):
                    out = slot(n)[:, a, :].rearrange("p (j k) -> p j k", j=nj)
                    nc.tensor.matmul(out[:, :, t * P:(t + 1) * P], r.identb[:],
                                     r.above[:, None, :].to_broadcast([P, nj, P]), start=True, stop=False,
                                     skip_group_check=True)
                for j in range(nj):
                    for a in range(2):
                        out = slot(n)[:, a, :].rearrange("p (j k) -> p j k", j=nj)
                        last = nc.tensor.matmul(out[:, j, :], QT[rows[a], c.par, j0 + j, t * P:(t + 1) * P],
                                                KT[rows[a], c.par, j0 + j, 0:(t + 1) * P],
                                                start=False, stop=True, skip_group_check=True)
                last.then_inc(filled[n], 1)

            def scores_unit(u, c):
                t, j0, nj = ST_UNITS[u]
                if u == 0:
                    pe.wait_ge(max_rows_in, c.count(96, 96))
                n, uses = ring.use(f"ST{u}", c)
                if some(uses):
                    pe.wait_ge(drained[n], uses)
                for a in range(2):
                    out = slot(n)[:, a, :].rearrange("p (j q) -> p j q", j=nj)
                    nc.tensor.matmul(out[:, :, 0:P], r.identb[:], r.later[:, None, :].to_broadcast([P, nj, P]),
                                     start=True, stop=False, skip_group_check=True)
                for j in range(nj):
                    for a in range(2):
                        out = slot(n)[:, a, :].rearrange("p (j q) -> p j q", j=nj)
                        last = nc.tensor.matmul(out[:, j, :], KT[rows_m[a], c.par, j0 + j, t * P:(t + 1) * P],
                                                QT[rows_m[a], c.par, j0 + j, t * P:S], start=False, stop=True,
                                                skip_group_check=True)
                last.then_inc(filled[n], 1)

            def values(half, s, c):
                if s == 0:
                    pe.wait_ge(probs_ready, c.count(6, 3 * half + 3))
                    if some(due := c.count(2, half)):
                        pe.wait_ge(OT_ready, due)
                    if half == 0:
                        pe.wait_ge(V_ready, c.count(1, 1))
                for t in range(T):
                    for g in range(4):
                        h = 4 * (2 * half + s) + g
                        probs = (probs0 if t == 0 else probs1)[:, h, :]
                        last = nc.tensor.matmul(o_bank[32 * g:32 * g + 32, s * S + t * P:(s + 1) * S],
                                                V[:, c.par, t, h, :], probs, start=(t == 0), stop=(t == 1),
                                                skip_group_check=True)
                if s == 1:
                    last.then_inc(pv_done, 1)

            def transpose_attn(c):
                pe.wait_ge(attn_ready, c.count(1, 1))
                if some(due := c.count(1)):
                    pe.wait_ge(attnT_ready, due)
                for t in range(T):
                    last = nc.tensor.transpose(at_ps[:, t * P:(t + 1) * P],
                                               attn[:, t].rearrange("p h d -> p (h d)"), r.identf[:])
                last.then_inc(at_done, 1)

            def project(c):
                pe.wait_ge(attnT_ready, c.count(1, 1))
                n, uses = ring.use("PR", c)
                if some(uses):
                    pe.wait_ge(drained[n], uses)
                for t in range(T):
                    last = nc.tensor.matmul(slot(n)[:, 0, t * D:(t + 1) * D], attnT[:, t * P:(t + 1) * P],
                                            wout[:], start=True, stop=True)
                last.then_inc(filled[n], 1)

            def transpose_z2(c):
                pe.wait_ge(z2_ready, c.count(1, 1))
                n, uses = ring.use("Z2", c)
                if some(uses):
                    pe.wait_ge(drained[n], uses)
                for t in range(T):
                    last = nc.tensor.transpose(slot(n)[:, 0, t * P:(t + 1) * P], z2[:, c.par, t, :], r.identf[:])
                last.then_inc(filled[n], 1)

            def router(c):
                pe.wait_ge(h2T_ready, c.count(1, 1))
                n, uses = ring.use("LG", c)
                if some(uses):
                    pe.wait_ge(drained[n], uses)
                for t in range(T):
                    last = nc.tensor.matmul(slot(n)[:, 0, t * E:(t + 1) * E], h2T[:, t * P:(t + 1) * P],
                                            wgate[:], start=True, stop=True)
                last.then_inc(filled[n], 1)

            def counts(c):
                pe.wait_ge(chosen_ready, c.count(1, 1))
                n, uses = ring.use("CM", c)
                if some(uses):
                    pe.wait_ge(drained[n], uses)
                out = slot(n)[:, 0, :]
                nc.tensor.matmul(out[:, 0:E], r.upto[:], chosen[:, 0, :], start=True, stop=True)
                nc.tensor.matmul(out[:, E:2 * E], r.ones[:], chosen[:, 0, :], start=True, stop=False)
                nc.tensor.matmul(out[:, E:2 * E], r.upto[:], chosen[:, 1, :], start=False, stop=True)
                nc.tensor.matmul(out[:, 2 * E:3 * E], r.ones[:], chosen[:, 0, :], start=True, stop=False)
                last = nc.tensor.matmul(out[:, 2 * E:3 * E], r.ones[:], chosen[:, 1, :], start=False, stop=True)
                last.then_inc(filled[n], 1)

            def transpose_stack(name, side, c):
                if name == "QT":
                    pe.wait_ge(part3_ready, c.count(1, 1))
                n, uses = ring.use(name, c)
                if some(uses):
                    pe.wait_ge(drained[n], uses)
                out = slot(n).bitcast(BF16)
                for t in range(T):
                    for j in range(JP):
                        src = stack[:, c.par, side, t * H + 2 * j:t * H + 2 * j + 2, :, :]
                        last = nc.tensor.transpose(out[:, t, j * P:(j + 1) * P],
                                                   src.rearrange("p h s d -> p (h s d)"), r.identb[:])
                last.then_inc(filled[n], 1)

            def transpose_maxima(c):
                due = computed(pe, c.count(1, 1))
                n, uses = ring.use("MT", c)
                uses = computed(pe, uses)
                pe.wait_ge(consts_ready, 2)
                pe.wait_ge(m_ready, due)
                if some(uses):
                    pe.wait_ge(drained[n], uses)
                out = slot(n).bitcast(BF16)
                for t in range(T):
                    last = nc.tensor.transpose(out[0:2 * NMAX * JP, 0, t * P:(t + 1) * P],
                                               mparts[:, t].rearrange("p a k j -> p (a k j)"), r.identb[:])
                last.then_inc(filled[n], 1)

            def body(b):
                for u in range(6):
                    if (b + 1).live():
                        maxima_unit(u, b + 1)
                    if u == 5 and (b + 3).live():
                        transpose_z(b + 3)
                    if b.live():
                        scores_unit(u, b)
                    if u == 2 and (b + -1).live():
                        transpose_attn(b + -1)
                    if u == 3 and (b + -1).live():
                        project(b + -1)
                    if u in (3, 4) and b.live():
                        values(0, u - 3, b)
                if (b + 2).live():
                    transpose_stack("QT", 0, b + 2)
                    transpose_stack("KT", 1, b + 2)
                if ffn and (b + -1).live():
                    transpose_z2(b + -1)
                if b.live():
                    values(1, 0, b)
                if (b + 1).live():
                    transpose_maxima(b + 1)
                if b.live():
                    values(1, 1, b)
                if (b + 3).live():
                    qkv(b + 3)
                if ffn and (b + -2).live():
                    counts(b + -2)
                if ffn and (b + -1).live():
                    router(b + -1)
                if b.live():
                    transposed_values(b)

            iterations(pe, body)

        @block.scalar
        def _(act):
            act.wait_ge(loaded, 16 * n_loads)
            act.wait_ge(consts_ready, 3 if ffn else 2)

            def copy_hT(c):
                act.wait_ge(zt_done, c.count(1, 1))
                if ffn:
                    nc.scalar.activation(hT[:], zt_ps, ACT.Identity, scale=g1[:], bias=b1[:]).then_inc(hT_ready, 1)
                else:
                    nc.scalar.activation(hT[:], zt_ps, ACT.Copy).then_inc(hT_ready, 1)

            def copy_qkv(c):
                n, uses = ring.use("QKV", c)
                act.wait_ge(filled[n], uses + 1)
                if some(due := c.count(1)):
                    act.wait_ge(rest_ready, due)
                if some(due := c.count(1, -1)):
                    act.wait_ge(V_ready, due)
                nc.scalar.activation(qk[:].rearrange("p k (t h) d -> p t k (h d)", t=T),
                                     slot(n)[:, :, 0:2 * D].rearrange("p t (k n) -> p t k n", k=2),
                                     ACT.Copy).then_inc(qk_copied, 1)
                nc.scalar.activation(vraw[:, c.par], slot(n)[:, :, 2 * D:3 * D], ACT.Copy).then_inc(drained[n], 1)

            def exponentials(u, c):
                t, j0, nj = ST_UNITS[u]
                n, uses = ring.use(f"ST{u}", c)
                act.wait_ge(filled[n], uses + 1)
                if some(due := c.count(2, -1 + u // 3)):
                    act.wait_ge(pv_done, due)
                dst = (probs0 if t == 0 else probs1)[:, 2 * j0:2 * (j0 + nj), :].rearrange("p (j a) q -> p a j q", a=2)
                nc.scalar.activation(dst, slot(n).rearrange("p a (j q) -> p a j q", j=nj), ACT.Exp,
                                     scale=SCALE).then_inc(probs_ready, 1)
                act.drain().then_inc(drained[n], 1)

            def first_part(c):
                act.wait_ge(rotated if ffn else qk_copied, c.count(1, 1))
                nc.scalar.activation(stack[:, c.par, 0, :, 0:3, :],
                                     qk[:, 0, :, None, :].to_broadcast([P, T * H, 3, HD]), ACT.Copy)
                nc.scalar.activation(stack[:, c.par, 1, :, 0:7:3, :],
                                     qk[:, 1, :, None, :].to_broadcast([P, T * H, 3, HD]),
                                     ACT.Copy).then_inc(part1_ready, 1)

            def second_part(c):
                act.wait_ge(rest_ready, c.count(1, 1))
                nc.scalar.activation(stack[:, c.par, 0, :, 3:6, :],
                                     residual[:, 0, :, None, :].to_broadcast([P, T * H, 3, HD]), ACT.Copy)
                nc.scalar.activation(stack[:, c.par, 1, :, 1:5:3, :],
                                     residual[:, 1, :, None, :].to_broadcast([P, T * H, 2, HD]),
                                     ACT.Copy).then_inc(part2_ready, 1)

            def copy_attnT(c):
                act.wait_ge(at_done, c.count(1, 1))
                if (c + -1).live():
                    k, uses = ring.use("PR", c + -1)
                    act.wait_ge(filled[k], uses + 1)
                nc.scalar.activation(attnT[:], at_ps, ACT.Copy).then_inc(attnT_ready, 1)

            def copy_values(half, c):
                act.wait_ge(pv_done, c.count(2, half + 1))
                if half == 0 and (c + -1).live():
                    k, uses = ring.use("OT", c + -1)
                    act.wait_ge(filled[k], uses + 1)
                nc.scalar.activation(OT[:, 2 * half:2 * half + 2, :].rearrange("p s q -> p (s q)"), o_bank,
                                     ACT.Copy).then_inc(OT_ready, 1)

            def copy_h2T(c):
                n, uses = ring.use("Z2", c)
                act.wait_ge(filled[n], uses + 1)
                if (c + -1).live():
                    k, uses = ring.use("LG", c + -1)
                    act.wait_ge(filled[k], uses + 1)
                nc.scalar.activation(h2T[:], slot(n)[:, 0, 0:S], ACT.Identity, scale=g2[:],
                                     bias=b2[:]).then_inc(h2T_ready, 1)
                act.drain().then_inc(drained[n], 1)

            def gate_exp(c):
                act.wait_ge(shift_ready, c.count(1, 1))
                nc.scalar.activation(gexp[:], lshift[:], ACT.Exp).then_inc(gexp_ready, 1)

            def copy_stack(name, dst, done, c):
                n, uses = ring.use(name, c)
                act.wait_ge(filled[n], uses + 1)
                nc.scalar.activation(dst.rearrange("p j (t q) -> p t j q", t=T),
                                     slot(n).bitcast(BF16).rearrange("p t (j q) -> p t j q", j=JP),
                                     ACT.Copy).then_inc(done, 1)
                act.drain().then_inc(drained[n], 1)

            def place_V(c):
                if some(due := c.count(2, -2)):
                    act.wait_ge(pv_done, due)
                nc.scalar.activation(V[:, c.par, :, :, 0:HD], vraw[:, c.par].rearrange("p t (h d) -> p t h d", d=HD),
                                     ACT.Copy).then_inc(V_ready, 1)

            def body(b):
                if b.live():
                    exponentials(0, b)
                    exponentials(1, b)
                if (b + 2).live():
                    first_part(b + 2)
                if b.live():
                    exponentials(2, b)
                if (b + -1).live():
                    copy_attnT(b + -1)
                if b.live():
                    exponentials(3, b)
                if (b + 2).live():
                    second_part(b + 2)
                if b.live():
                    copy_values(0, b)
                    exponentials(4, b)
                if (b + 3).live():
                    copy_hT(b + 3)
                if b.live():
                    exponentials(5, b)
                if (b + 2).live():
                    copy_stack("QT", QT[:, (b + 2).par], QT_ready, b + 2)
                    copy_stack("KT", KT[:, (b + 2).par], KT_ready, b + 2)
                if ffn and (b + -1).live():
                    copy_h2T(b + -1)
                if b.live():
                    copy_values(1, b)
                if (b + 3).live():
                    copy_qkv(b + 3)
                if (b + 2).live():
                    place_V(b + 2)
                if ffn and (b + -1).live():
                    gate_exp(b + -1)

            iterations(act, body)

        @block.vector
        def _(dve):
            for par in range(2):
                nc.vector.memset(stack[:, par], 0.0)
                nc.vector.memset(V[:, par], 0.0)
            dve.drain()
            for par in range(2):
                nc.vector.memset(stack[:, par, 1, :, 7, 0:NMAX], 1.0)
                last = nc.vector.memset(V[:, par, :, :, HD:HD + 1], 1.0)
            last.then_inc(consts_ready, 2)
            if ffn:
                nc.vector.memset(carry[:], 0.0).then_inc(consts_ready, 1)
            dve.wait_ge(loaded, 16 * n_loads)

            def tokens(buf, c, t):
                return buf[:, bass.ds(c.count(S, t * D), D)]

            def ln_stats(k, src):
                for t in range(T):
                    nc.vector.bn_stats(stats[:, k, t, :], src(t))
                dve.drain()
                for t in range(T):
                    nc.vector.bn_aggr(mv[:, k, t, :], stats[:, k, t, :])
                dve.drain()
                nc.vector.tensor_scalar(var_eps[:, k, :], mv[:, k, :, 1], EPS, None,
                                        ALU.add).then_inc(var_ready[k], 1)

            def ln_apply(k, c, dst, src):
                dve.wait_ge(rstd_ready[k], c.count(1, 1))
                mean_of = 0 if k == 1 else k
                for t in range(T):
                    last = nc.vector.tensor_scalar(dst(t), src(t), mv[:, mean_of, t, 0:1], rstd[:, k, t:t + 1],
                                                   ALU.subtract, ALU.mult)
                return last

            def combine(c):
                dve.wait_ge(gathered[c.par], c.of_parity(16 * T * TOPK))
                for k in range(TOPK):
                    for t in range(T):
                        n = t * TOPK + k
                        nc.vector.scalar_tensor_tensor(moe[:, t, :], eo[:, c.par, n, :],
                                                       r.gate[:, bass.ds(c.count(T * TOPK, n), 1)],
                                                       tokens(r.Y, c, t) if k == 0 else moe[:, t, :],
                                                       ALU.mult, ALU.add)
                    dve.drain()
                for t in range(T):
                    last = nc.vector.scalar_tensor_tensor(tokens(r.X, c, t), moe[:, t, :], 0.5, tokens(r.X, c, t),
                                                          ALU.mult, ALU.add)
                last.then_inc(combined, 1)
                dve.drain()

            def norm_values(c):
                dve.drain()
                n, uses = ring.use("OT", c)
                dve.wait_ge(filled[n], uses + 1)
                src = slot(n).rearrange("p t (h r) -> p t h r", r=32)
                nc.vector.reciprocal(rden[:], src[:, :, :, HD])
                dve.drain()
                if some(due := c.count(1)):
                    dve.wait_ge(at_done, due)
                for t in range(T):
                    last = nc.vector.tensor_tensor(attn[:, t], src[:, t, :, 0:HD],
                                                   rden[:, t, :, None].to_broadcast([P, H, HD]), ALU.mult)
                last.then_inc(attn_ready, 1)
                dve.drain().then_inc(drained[n], 1)

            def maxima(u, c):
                t, j0, nj = S_UNITS[u]
                n, uses = ring.use(f"S{u}", c)
                dve.wait_ge(filled[n], uses + 1)
                dst = nmax[:, t * H:(t + 1) * H].rearrange("p (j a) -> p a j", a=2)[:, :, j0:j0 + nj]
                nc.vector.tensor_reduce(dst, slot(n).rearrange("p a (j k) -> p a j k", j=nj), AX.X, ALU.max,
                                        negate=True).then_inc(drained[n], 1)

            def maxima_parts(c):
                m = [mparts[:, :, :, k, :] for k in range(NMAX)]
                whole = nmax[:].rearrange("p (t j a) -> p t a j", t=T, a=2)
                left = nmax_rest[:].rearrange("p (t j a) -> p t a j", t=T, a=2)
                dve.drain()
                nc.vector.tensor_copy(m[0], whole)
                dve.drain()
                nc.vector.tensor_tensor(left, whole, m[0], ALU.subtract)
                dve.drain()
                nc.vector.tensor_copy(m[1], left)
                dve.drain()
                nc.vector.tensor_tensor(m[2], left, m[1], ALU.subtract).then_inc(m_ready, 1)

            def rest(c):
                dve.wait_ge(part1_ready, c.count(1, 1))
                nc.vector.tensor_tensor(residual[:].rearrange("p k h d -> p (k h) d"),
                                        qk[:].rearrange("p k h d -> p (k h) d"),
                                        stack[:, c.par].rearrange("p k h s d -> p (k h) s d")[:, :, 0, :],
                                        ALU.subtract).then_inc(rest_ready, 1)

            def third_part(c):
                dve.wait_ge(part2_ready, c.count(1, 1))
                nc.vector.tensor_tensor(stack[:, c.par, 0, :, 6, :], residual[:, 0],
                                        stack[:, c.par, 0, :, 4, :], ALU.subtract)
                nc.vector.tensor_tensor(stack[:, c.par, 1, :, 2:6:3, :],
                                        residual[:, 1, :, None, :].to_broadcast([P, T * H, 2, HD]),
                                        stack[:, c.par, 1, :, 4:5, :].to_broadcast([P, T * H, 2, HD]),
                                        ALU.subtract).then_inc(part3_ready, 1)

            def copy_mT(c):
                n, uses = ring.use("MT", c)
                dve.wait_ge(filled[n], uses + 1)
                if some(due := c.count(96)):
                    dve.wait_ge(max_rows_in, due)
                nc.vector.tensor_copy(mT[:], slot(n).bitcast(BF16)[0:2 * NMAX * JP, 0, 0:S]).then_inc(mT_ready, 1)
                dve.drain().then_inc(drained[n], 1)

            def residual_sum(c):
                n, uses = ring.use("PR", c)
                dve.wait_ge(filled[n], uses + 1)
                out = r.Y if ffn else r.X
                for t in range(T):
                    last = nc.vector.tensor_tensor(tokens(out, c, t), tokens(out, c, t),
                                                   slot(n)[:, 0, t * D:(t + 1) * D], ALU.add)
                last.then_inc(drained[n], 1)
                dve.drain()
                if not ffn:
                    for t in range(T):
                        nc.vector.tensor_tensor(tokens(out, c, t), tokens(out, c, t), bias[:], ALU.add)

            def route_shift(c):
                n, uses = ring.use("LG", c)
                dve.wait_ge(filled[n], uses + 1)
                src = slot(n)[:, 0, 0:T * E].rearrange("p (t e) -> p t e", e=E)
                nc.vector.tensor_reduce(nlmax[:], src, AX.X, ALU.max, negate=True)
                dve.drain()
                nc.vector.tensor_tensor(lshift[:], src, nlmax[:, :, None].to_broadcast([P, T, E]),
                                        ALU.add).then_inc(shift_ready, 1)
                dve.drain().then_inc(drained[n], 1)

            def route_choose(c):
                dve.wait_ge(gexp_ready, c.count(1, 1))
                nc.vector.tensor_reduce(gsum[:], gexp[:], AX.X, ALU.add)
                dve.drain()
                nc.vector.reciprocal(gsum[:], gsum[:])
                dve.drain()
                nc.vector.tensor_tensor(gates[:], gexp[:], gsum[:, :, None].to_broadcast([P, T, E]), ALU.mult)
                dve.drain()
                for t in range(T):
                    nc.vector.max(top[:, t, :], gates[:, t, :])
                dve.drain()
                for t in range(T):
                    nc.vector.max_index(top_at[:, t, :], top[:, t, :], gates[:, t, :])
                dve.drain()
                nc.vector.tensor_copy(expert[:], top_at[:, :, 0:TOPK])
                dve.drain()
                nc.vector.tensor_tensor(onehot[:].rearrange("p t k e -> p (t k) e"),
                                        r.iota8[:, None, :].to_broadcast([P, T * TOPK, E]),
                                        expert[:].rearrange("p t k -> p (t k)")[:, :, None]
                                        .to_broadcast([P, T * TOPK, E]), ALU.is_equal)
                dve.drain()
                nc.vector.tensor_tensor(chosen[:], onehot[:, :, 0, :], onehot[:, :, 1, :],
                                        ALU.add).then_inc(chosen_ready, 1)

            def route_place(c):
                n, uses = ring.use("CM", c)
                dve.wait_ge(filled[n], uses + 1)
                src = slot(n)[:, 0, :]
                nc.vector.tensor_tensor(count[:], src[:, 0:T * E].rearrange("p (t e) -> p t e", e=E),
                                        carry[:, None, :].to_broadcast([P, T, E]), ALU.add)
                dve.drain()
                nc.vector.tensor_tensor(carry[:], src[:, T * E:(T + 1) * E], carry[:],
                                        ALU.add).then_inc(drained[n], 1)
                nc.vector.tensor_tensor(picked[:], onehot[:],
                                        count[:, :, None, :].to_broadcast([P, T, TOPK, E]), ALU.mult)
                dve.drain()
                nc.vector.tensor_reduce(pos[:].rearrange("p (t k) -> p t k", t=T), picked[:], AX.X, ALU.add)
                dve.drain()
                nc.vector.tensor_scalar(over[:], pos[:], CAP + 0.5, DROP, ALU.is_gt, ALU.mult)
                nc.vector.tensor_scalar(place[:], pos[:], float(CAP), -1.0, ALU.min, ALU.add)
                dve.drain()
                nc.vector.scalar_tensor_tensor(place[:], expert[:].rearrange("p t k -> p (t k)"), float(CAP),
                                               place[:], ALU.mult, ALU.add)
                nc.vector.tensor_scalar(pos[:], over[:], 0.0, None, ALU.is_equal)
                dve.drain()
                if some(due := (c + -2).of_parity(16 * T * TOPK)):
                    dve.wait_ge(sent[c.par], due)
                gate_at = bass.ds(c.count(T * TOPK), T * TOPK)
                nc.vector.tensor_tensor(r.gate[:, gate_at].rearrange("p (t k) -> p t k", t=T),
                                        pos[:].rearrange("p (t k) -> p t k", t=T), top[:, :, 0:TOPK], ALU.mult)
                nc.vector.tensor_copy(r.slots[:, gate_at], place[:])
                nc.vector.tensor_tensor(send_to[:, c.par, :], place[:], over[:], ALU.add).then_inc(send_ready, 1)
                dve.drain()

            def body(b):
                if (b + -1).live():
                    norm_values(b + -1)
                if (b + 1).live():
                    maxima(0, b + 1)
                    maxima(1, b + 1)
                if (b + 1).live():
                    maxima(2, b + 1)
                if (b + 2).live():
                    rest(b + 2)
                if (b + 1).live():
                    maxima(3, b + 1)
                if (b + -1).live():
                    residual_sum(b + -1)
                    if ffn:
                        ln_stats(2, lambda t: tokens(r.Y, b + -1, t))
                if (b + 1).live():
                    maxima(4, b + 1)
                if (b + 2).live():
                    third_part(b + 2)
                if (b + 1).live():
                    maxima(5, b + 1)
                    maxima_parts(b + 1)
                if ffn and (b + -1).live():
                    if some(due := (b + -3).of_parity(16 * T * TOPK)):
                        dve.wait_ge(sent[(b + -1).par], due)
                    ln_apply(2, b + -1, lambda t: z2[:, (b + -1).par, t, :],
                             lambda t: tokens(r.Y, b + -1, t)).then_inc(z2_ready, 1)
                if (b + 1).live():
                    copy_mT(b + 1)
                if ffn and (b + -2).live():
                    route_choose(b + -2)
                if not ffn and (b + 4).live():
                    combine(b + 4)
                if (b + 4).live():
                    dve.drain()
                    if ffn and r.loads_x:
                        dve.wait_ge(x_loaded[(b + 4).par], (b + 4).of_parity(16))
                    ln_stats(0, lambda t: tokens(r.X, b + 4, t))
                if ffn and (b + -2).live():
                    route_place(b + -2)
                if ffn and (b + -1).live():
                    route_shift(b + -1)
                if (b + 4).live():
                    if some(due := (b + 4).count(1, -1)):
                        dve.wait_ge(zt_done, due)
                    if ffn:
                        ln_apply(0, b + 4, lambda t: tokens(r.Y, b + 4, t), lambda t: tokens(r.X, b + 4, t))
                    ln_apply(1 if ffn else 0, b + 4, lambda t: z[:, (b + 4).par, t, :],
                             lambda t: tokens(r.X, b + 4, t)).then_inc(z_ready, 1)

            iterations(dve, body)

        @block.gpsimd
        def _(pool):
            pool.sem_inc(begun, 1)
            last_slot = pool.to_reg(E * CAP - 1)

            def root(k, c):
                pool.wait_ge(var_ready[k], c.count(1, 1))
                nc.gpsimd.tensor_tensor(rstd[:, k, :], var_eps[:, k, :], r.minus_half[:, 0:T],
                                        ALU.pow).then_inc(rstd_ready[k], 1)

            def root_again(c):
                first, second, v = rstd[:, 0, :], rstd[:, 1, :], again[:]
                pool.drain()
                nc.gpsimd.tensor_tensor(v, mv[:, 0, :, 1], first, ALU.mult)
                pool.drain()
                nc.gpsimd.tensor_tensor(v, v, first, ALU.mult)
                pool.drain()
                nc.gpsimd.tensor_scalar(v, v, EPS, None, ALU.add)
                pool.drain()
                nc.gpsimd.tensor_tensor(v, v, r.minus_half[:, 0:T], ALU.pow)
                pool.drain()
                nc.gpsimd.tensor_tensor(second, v, first, ALU.mult).then_inc(rstd_ready[1], 1)

            def rotate(c):
                pool.wait_ge(qk_copied, c.count(1, 1))
                for k in range(2):
                    for t in range(T):
                        src = qk[:, k, t * H:(t + 1) * H, :]
                        nc.gpsimd.tensor_tensor(swapped[:, t, k * H:(k + 1) * H, :]
                                                .rearrange("p h (u e) -> p h u e", u=2),
                                                src.rearrange("p h (u e) -> p h u e", u=2)[:, :, ::-1, :],
                                                sin[:, t, None, :].to_broadcast([P, H, HD])
                                                .rearrange("p h (u e) -> p h u e", u=2), ALU.mult)
                pool.drain()
                for k in range(2):
                    for t in range(T):
                        src = qk[:, k, t * H:(t + 1) * H, :]
                        nc.gpsimd.tensor_tensor(src, src, cos[:, t, None, :].to_broadcast([P, H, HD]), ALU.mult)
                pool.drain()
                for k in range(2):
                    for t in range(T):
                        src = qk[:, k, t * H:(t + 1) * H, :]
                        last = nc.gpsimd.tensor_tensor(src, src, swapped[:, t, k * H:(k + 1) * H, :], ALU.add)
                last.then_inc(rotated, 1)

            def send(c):
                due = computed(pool, c.count(1, 1))
                pool.wait_ge(begun, 1)
                pool.wait_ge(send_ready, due)
                for t in range(T):
                    for k in range(TOPK):
                        n = t * TOPK + k
                        nc.gpsimd.indirect_dma_start(
                            out=r.expert_in, out_offset=bass.IndirectOffsetOnAxis(send_to[:, c.par, n:n + 1], 0),
                            in_=z2[:, c.par, t, :], in_offset=None, bounds_check=last_slot,
                            oob_is_err=False).then_inc(sent[c.par], 16)

            def gather(c):
                if some(due := computed(pool, c.count(1, -1))):
                    pool.wait_ge(begun, 1)
                    pool.wait_ge(combined, due)
                if some(due := (c + -2).of_parity(16 * T * TOPK)):
                    pool.wait_ge(gathered[c.par], due)
                nc.gpsimd.tensor_copy(read_at[:, c.par, :],
                                      r.slots[:, bass.ds(c.count(T * TOPK), T * TOPK)]).then_inc(index_ready, 1)
                due = computed(pool, c.count(1, 1))
                pool.wait_ge(begun, 1)
                pool.wait_ge(index_ready, due)
                for n in range(T * TOPK):
                    nc.gpsimd.indirect_dma_start(
                        out=eo[:, c.par, n, :], out_offset=None, in_=r.expert_out,
                        in_offset=bass.IndirectOffsetOnAxis(read_at[:, c.par, n:n + 1], 0),
                        bounds_check=last_slot, oob_is_err=False).then_inc(gathered[c.par], 16)

            def body(b):
                if not ffn and (b + 5).live():
                    gather(b + 5)
                if ffn and (b + -1).live():
                    root(2, b + -1)
                if (b + 4).live():
                    root(0, b + 4)
                    if ffn:
                        root_again(b + 4)
                if ffn and (b + 3).live():
                    rotate(b + 3)
                if ffn and (b + -2).live():
                    send(b + -2)

            iterations(pool, body)
            if ffn:
                for par in range(2):
                    pool.wait_ge(sent[par], 16 * T * TOPK * NB // 2)
    give_back(nc, sems)



def expert_pass(nc, r):
    per_expert = CAP // GROUP
    groups = 2 * per_expert
    pairs = E // 2
    sems = []
    with ExitStack() as ctx:
        def sb(name, shape, dt=F32):
            return ctx.enter_context(nc.sbuf_tensor(f"{name}_{r.tag}", shape, dt))

        def sem(name):
            return new_semaphore(nc, sems, f"{name}_{r.tag}")

        psum = ctx.enter_context(nc.psum_tensor(f"psum_{r.tag}", [P, 8, 512], F32))
        xt_ps, back_ps = psum[:, 0, :], psum[:, 1, :]

        def hidden_ps(k):
            return psum[:, 2 + k % 4, :]

        def out_ps(n):
            return psum[:, 6 + n % 2, :]

        w1 = sb("w1", [D, 2, F])
        w2 = sb("w2", [P, 2, FC, D])
        bias1 = sb("bias1", [P, 2, FC])
        bias2 = sb("bias2", [D, 2])
        gain = sb("gain", [D, 1])
        shift = sb("shift", [D, 1])
        rows = sb("rows", [P, 2, 4, D])
        xT = sb("xT", [D, 2, GROUP])
        hidden = sb("hidden", [P, 2, FC, GROUP])
        outT = sb("outT", [D, GROUP])
        back = sb("back", [P, 2, 4, D])

        loaded = sem("loaded")
        weights = [sem(f"weights{n}") for n in range(2)]
        rows_in = [sem(f"rows_in{n}") for n in range(2)]
        xt_done = sem("xt_done")
        xT_ready = sem("xT_ready")
        hidden_done = sem("hidden_done")
        gelu_ready = sem("gelu_ready")
        out_done = sem("out_done")
        outT_ready = sem("outT_ready")
        back_done = sem("back_done")
        back_ready = sem("back_ready")
        stored = [sem(f"stored{n}") for n in range(2)]
        sp_begun = sem("sp_begun")
        block = ctx.enter_context(nc.Block())

        class Group:

            def __init__(self, reg, const):
                self.reg, self.const, self.par = reg, const, const % 2

            def count(self, per, extra=0):
                fixed = per * self.const + extra
                return fixed if self.reg is None else self.reg * (groups * per) + fixed

            def of_parity(self, per):
                fixed = per * ((self.const - self.par) // 2 + 1)
                return fixed if self.reg is None else self.reg * (groups // 2 * per) + fixed

        total = pairs * groups

        def all_groups(eng, body):
            for g in range(-1, groups):
                body(Group(None, g), g >= 0, True)
            with eng.Fori(1, pairs - 1) as i:
                for g in range(groups):
                    body(Group(i, g), True, True)
            for g in range(total - groups, total + 1):
                body(Group(None, g), g < total, g + 1 < total)

        @block.sync
        def _(sp):
            sp.sem_inc(sp_begun, 1)
            sp.dma_start(gain[:], r.ln2_g).then_inc(loaded, 16)
            sp.dma_start(shift[:], r.ln2_b).then_inc(loaded, 16)

            def fetch(g):
                if some(due := computed(sp, g.count(1, -1))):
                    sp.wait_ge(sp_begun, 1)
                    sp.wait_ge(xt_done, due)
                if some(due := g.of_parity(16) - 16):
                    sp.wait_ge(rows_in[g.par], due)
                sp.dma_start(rows[:, g.par], r.expert_in[bass.ds(g.count(GROUP), GROUP), :]
                             .rearrange("(p c) d -> p c d", c=4)).then_inc(rows_in[g.par], 16)

            def fetch_weights(e, experts_before):
                at = e % 2
                n = experts_before
                if some(due := computed(sp, n * per_expert - per_expert)):
                    sp.wait_ge(sp_begun, 1)
                    sp.wait_ge(out_done, due)
                sp.dma_start(w1[:, at], r.w1[bass.ds(n * D, D), :]).then_inc(weights[at], 16)
                sp.dma_start(w2[:, at], r.w2[bass.ds(n * F, F), :].rearrange("(c p) d -> p c d", p=P)
                             ).then_inc(weights[at], 16)
                sp.dma_start(bias1[:, at], r.bias1[bass.ds(n * P, P), :]).then_inc(weights[at], 16)
                sp.dma_start(bias2[:, at:at + 1], r.bias2[bass.ds(n * D, D), :]).then_inc(weights[at], 16)

            def store(g):
                due = computed(sp, g.count(1, 1))
                sp.wait_ge(sp_begun, 1)
                sp.wait_ge(back_ready, due)
                sp.dma_start(r.expert_out[bass.ds(g.count(GROUP), GROUP), :].rearrange("(p c) d -> p c d", c=4),
                             back[:, g.par]).then_inc(stored[g.par], 16)

            def step(g, ahead, weights_of):
                if weights_of is not None:
                    fetch_weights(*weights_of)
                if ahead:
                    fetch(Group(g.reg, g.const + 2))
                store(g)

            fetch_weights(0, 0)
            fetch(Group(None, 0))
            fetch(Group(None, 1))
            fetch_weights(1, 1)
            for g in range(groups):
                step(Group(None, g), True, (g // per_expert, g // per_expert + 2) if g % per_expert == 2 and False
                     else None)
                if g % per_expert == per_expert - 1:
                    fetch_weights(g // per_expert, g // per_expert + 2)
            with sp.Fori(1, pairs - 1) as i:
                for g in range(groups):
                    step(Group(i, g), True, None)
                    if g % per_expert == per_expert - 1:
                        fetch_weights(g // per_expert, i * 2 + (g // per_expert + 2))
            for g in range(total - groups, total):
                step(Group(None, g), g + 2 < total, None)
            for par in range(2):
                sp.wait_ge(stored[par], 16 * total // 2)

        def weights_count(g):
            return 64 * (g.const // groups + 1) if g.reg is None else g.reg * 64 + 64

        @block.tensor
        def _(pe):
            def transpose_in(g):
                pe.wait_ge(rows_in[g.par], g.of_parity(16))
                if some(due := g.count(1)):
                    pe.wait_ge(xT_ready, due)
                for c in range(4):
                    last = nc.tensor.transpose(xt_ps[:, c * P:(c + 1) * P], rows[:, g.par, c, :], r.identf[:])
                last.then_inc(xt_done, 1)

            def first_matrix(g, f):
                if f == 0:
                    if g.const % per_expert == 0:
                        pe.wait_ge(weights[g.const // per_expert % 2], weights_count(g))
                    pe.wait_ge(xT_ready, g.count(1, 1))
                if some(due := g.count(4, f + 1 - 4)):
                    pe.wait_ge(gelu_ready, due)
                at = g.const // per_expert % 2
                nc.tensor.matmul(hidden_ps(f), w1[:, at, f * P:(f + 1) * P], xT[:, g.par, :],
                                 start=True, stop=True).then_inc(hidden_done, 1)

            def second_matrix(g):
                if some(due := g.count(1, -1)):
                    pe.wait_ge(outT_ready, due)
                at = g.const // per_expert % 2
                for f in range(FC):
                    pe.wait_ge(gelu_ready, g.count(4, f + 1))
                    last = nc.tensor.matmul(out_ps(g.par), w2[:, at, f, :], hidden[:, g.par, f, :],
                                            start=(f == 0), stop=(f == FC - 1))
                last.then_inc(out_done, 1)

            def transpose_back(g):
                pe.wait_ge(outT_ready, g.count(1, 1))
                if some(due := g.count(1)):
                    pe.wait_ge(back_ready, due)
                for c in range(4):
                    last = nc.tensor.transpose(back_ps[:, c * P:(c + 1) * P], outT[:, c * P:(c + 1) * P],
                                               r.identf[:])
                last.then_inc(back_done, 1)

            def body(g, now, ahead):
                before = Group(g.reg, g.const - 1)
                behind = now and (g.reg is not None or g.const > 0) or not now and g.const == total
                if now:
                    first_matrix(g, 0)
                    first_matrix(g, 1)
                if behind:
                    transpose_back(before)
                if now:
                    first_matrix(g, 2)
                    first_matrix(g, 3)
                if ahead:
                    transpose_in(Group(g.reg, g.const + 1))
                if now:
                    second_matrix(g)

            all_groups(pe, body)

        @block.scalar
        def _(act):
            def body(g, now, ahead):
                if not now:
                    return
                at = g.const // per_expert % 2
                if g.const % per_expert == 0:
                    act.wait_ge(weights[g.const // per_expert % 2], weights_count(g))
                for f in range(FC):
                    act.wait_ge(hidden_done, g.count(4, f + 1))
                    if f == 0:
                        if some(due := g.count(1, -1)):
                            act.wait_ge(out_done, due)
                    nc.scalar.activation(hidden[:, g.par, f, :], hidden_ps(f), ACT.Gelu,
                                         bias=bias1[:, at, f:f + 1]).then_inc(gelu_ready, 1)

            all_groups(act, body)

        @block.vector
        def _(dve):
            dve.wait_ge(loaded, 32)

            def copy_in(g):
                dve.wait_ge(xt_done, g.count(1, 1))
                if some(due := g.count(4, -4)):
                    dve.wait_ge(hidden_done, due)
                nc.vector.tensor_scalar(xT[:, g.par, :], xt_ps, gain[:], shift[:], ALU.mult,
                                        ALU.add).then_inc(xT_ready, 1)

            def copy_out(g):
                dve.wait_ge(out_done, g.count(1, 1))
                if some(due := g.count(1)):
                    dve.wait_ge(back_done, due)
                at = g.const // per_expert % 2
                if g.const % per_expert == 0:
                    dve.wait_ge(weights[g.const // per_expert % 2], weights_count(g))
                nc.vector.tensor_scalar(outT[:], out_ps(g.par), bias2[:, at:at + 1], None,
                                        ALU.add).then_inc(outT_ready, 1)

            def copy_back(g):
                dve.wait_ge(back_done, g.count(1, 1))
                if some(due := Group(g.reg, g.const - 2).of_parity(16)):
                    dve.wait_ge(stored[g.par], due)
                nc.vector.tensor_copy(back[:, g.par].rearrange("p c d -> p (c d)"), back_ps).then_inc(back_ready, 1)

            def body(g, now, ahead):
                before = Group(g.reg, g.const - 1)
                behind = now and (g.reg is not None or g.const > 0) or not now and g.const == total
                if behind:
                    copy_back(before)
                if ahead:
                    copy_in(Group(g.reg, g.const + 1))
                if now:
                    copy_out(g)

            all_groups(dve, body)
    give_back(nc, sems)


def last_pass(nc, r):
    sems = []
    with ExitStack() as ctx:
        def sb(name, shape, dt=F32):
            return ctx.enter_context(nc.sbuf_tensor(f"{name}_{r.tag}", shape, dt))

        def sem(name):
            return new_semaphore(nc, sems, f"{name}_{r.tag}")

        K = T * TOPK
        eo = sb("eo", [P, 2, K, D])
        read_at = sb("read_at", [P, 2, K], I32)
        moe = sb("moe", [P, T, D])
        result = sb("result", [P, 2, T, D])
        index_ready = sem("index_ready")
        gathered = [sem(f"gathered{n}") for n in range(2)]
        combined = sem("combined")
        begun = sem("begun")
        sp_begun = sem("sp_begun")
        stored = [sem(f"stored{n}") for n in range(2)]
        block = ctx.enter_context(nc.Block())

        def sequences(eng, body):
            for c in range(4):
                body(Seq(None, c))
            with eng.Fori(2, NB // 2) as i:
                body(Seq(i, 0))
                body(Seq(i, 1))

        @block.gpsimd
        def _(pool):
            pool.sem_inc(begun, 1)
            last_slot = pool.to_reg(E * CAP - 1)

            def gather(c):
                if some(due := computed(pool, c.count(1, -1))):
                    pool.wait_ge(begun, 1)
                    pool.wait_ge(combined, due)
                if some(due := (c + -2).of_parity(16 * K)):
                    pool.wait_ge(gathered[c.par], due)
                nc.gpsimd.tensor_copy(read_at[:, c.par, :], r.slots[:, bass.ds(c.count(K), K)]).then_inc(index_ready, 1)
                due = computed(pool, c.count(1, 1))
                pool.wait_ge(begun, 1)
                pool.wait_ge(index_ready, due)
                for n in range(K):
                    nc.gpsimd.indirect_dma_start(
                        out=eo[:, c.par, n, :], out_offset=None, in_=r.expert_out,
                        in_offset=bass.IndirectOffsetOnAxis(read_at[:, c.par, n:n + 1], 0),
                        bounds_check=last_slot, oob_is_err=False).then_inc(gathered[c.par], 16)
            sequences(pool, gather)

        @block.vector
        def _(dve):
            def tokens(buf, c, t):
                return buf[:, bass.ds(c.count(S, t * D), D)]

            def combine(c):
                dve.wait_ge(gathered[c.par], c.of_parity(16 * K))
                if some(due := (c + -2).of_parity(16)):
                    dve.wait_ge(stored[c.par], due)
                for k in range(TOPK):
                    for t in range(T):
                        n = t * TOPK + k
                        nc.vector.scalar_tensor_tensor(moe[:, t, :], eo[:, c.par, n, :],
                                                       r.gate[:, bass.ds(c.count(K, n), 1)],
                                                       tokens(r.Y, c, t) if k == 0 else moe[:, t, :],
                                                       ALU.mult, ALU.add)
                    dve.drain()
                for t in range(T):
                    last = nc.vector.scalar_tensor_tensor(result[:, c.par, t, :], moe[:, t, :], 0.5,
                                                          tokens(r.X, c, t), ALU.mult, ALU.add)
                last.then_inc(combined, 1)
                dve.drain()
            sequences(dve, combine)

        @block.sync
        def _(sp):
            sp.sem_inc(sp_begun, 1)

            def store(c):
                due = computed(sp, c.count(1, 1))
                sp.wait_ge(sp_begun, 1)
                sp.wait_ge(combined, due)
                if some(due := (c + -2).of_parity(16)):
                    sp.wait_ge(stored[c.par], due)
                sp.dma_start(r.out[bass.ds(c.count(S), S), :].rearrange("(t p) d -> p t d", p=P),
                             result[:, c.par]).then_inc(stored[c.par], 16)
            sequences(sp, store)
            for par in range(2):
                sp.wait_ge(stored[par], 16 * NB // 2)
    give_back(nc, sems)


class Resident:
    pass


def macaron(nc, inp, out):
    r = Resident()
    col = lambda a: a.rearrange("(d a) -> d a", a=1)
    r.x = inp["L0_attn_x"].rearrange("b s d -> (b s) d")
    r.out = out.rearrange("b s d -> (b s) d")
    r.ln1_g, r.ln1_b = col(inp["L0_ffn_ln1_g"]), col(inp["L0_ffn_ln1_b"])
    r.ln2_g, r.ln2_b = col(inp["L0_ffn_ln2_g"]), col(inp["L0_ffn_ln2_b"])
    r.wgate, r.cos, r.sin = inp["L0_ffn_Wgate"], inp["rope_cos"], inp["rope_sin"]
    r.w1 = inp["L0_ffn_W1"].rearrange("e d f -> (e d) f")
    r.w2 = inp["L0_ffn_W2"].rearrange("e f d -> (e f) d")
    r.bias1 = inp["ffn_b1"]
    r.bias2 = inp["L0_ffn_b2"].rearrange("e (d a) -> (e d) a", a=1)
    r.expert_in = nc.dram_tensor("expert_in", [E * CAP, D], F32, kind="Internal").ap()
    r.expert_out = nc.dram_tensor("expert_out", [E * CAP, D], F32, kind="Internal").ap()
    with ExitStack() as ctx:
        def sb(name, shape, dt=F32):
            return ctx.enter_context(nc.sbuf_tensor(name, shape, dt))

        r.X = sb("X", [P, NB * S])
        r.Y = sb("Y", [P, NB * S])
        r.gate = sb("gate", [P, NB * T * TOPK])
        r.slots = sb("slots", [P, NB * T * TOPK], I32)
        r.identf = sb("identf", [P, P])
        r.identb = sb("identb", [P, P], BF16)
        r.above = sb("above", [P, P], BF16)
        r.later = sb("later", [P, P], BF16)
        r.upto = sb("upto", [P, P], BF16)
        r.ones = sb("ones", [P, P], BF16)
        r.iota8 = sb("iota8", [P, E])
        r.minus_half = sb("minus_half", [P, 2])
        iota_i = sb("iota_i", [P, E], I32)
        zeros = sb("zeros", [P, 8, D])
        made, zeroed = (nc.alloc_semaphore(name=n) for n in ("made", "zeroed"))
        with nc.Block() as block:
            @block.gpsimd
            def _(pool):
                nc.gpsimd.memset(zeros[:], 0.0).then_inc(made, 1)
                for buf, value in ((r.identf, 0.0), (r.identb, 0.0), (r.above, 0.0), (r.later, 0.0),
                                   (r.upto, 1.0), (r.ones, 1.0),
                                   (r.minus_half, -0.5)):
                    nc.gpsimd.memset(buf[:], value)
                nc.gpsimd.iota(iota_i[:], pattern=[[1, E]], base=0, channel_multiplier=0)
                pool.drain()
                for buf in (r.identf, r.identb):
                    nc.gpsimd.affine_select(out=buf[:], in_=buf[:], compare_op=ALU.not_equal, fill=1.0, base=0,
                                            pattern=[[-1, P]], channel_multiplier=1)
                nc.gpsimd.affine_select(out=r.above[:], in_=r.above[:], compare_op=ALU.is_ge, fill=-BIG, base=0,
                                        pattern=[[-1, P]], channel_multiplier=1)
                nc.gpsimd.affine_select(out=r.later[:], in_=r.later[:], compare_op=ALU.is_ge, fill=-BIG, base=0,
                                        pattern=[[1, P]], channel_multiplier=-1)
                nc.gpsimd.affine_select(out=r.upto[:], in_=r.upto[:], compare_op=ALU.is_ge, fill=0.0, base=0,
                                        pattern=[[1, P]], channel_multiplier=-1)
                nc.gpsimd.tensor_copy(r.iota8[:], iota_i[:])
                pool.drain()

            @block.sync
            def _(sp):
                sp.wait_ge(made, 1)
                for n in range(E * CAP // (8 * P)):
                    sp.dma_start(r.expert_in[n * 8 * P:(n + 1) * 8 * P, :].rearrange("(p c) d -> p c d", c=8),
                                 zeros[:]).then_inc(zeroed, 16)
                sp.wait_ge(zeroed, 16 * (E * CAP // (8 * P)))

        r.tag, r.loads_x, r.wqkv, r.wout = "f1", True, inp["ffn_Wqkv"], inp["L0_ffn_Wproj"]
        attention_pass(nc, "ffn", r)
        r.tag = "e1"
        expert_pass(nc, r)
        r.tag, r.loads_x, r.wqkv, r.wout = "p", False, inp["attn_Wqkv"], inp["L0_attn_Wo"]
        r.bias = inp["L0_attn_bo"].rearrange("(a d) -> a d", a=1)
        attention_pass(nc, "plain", r)
        r.tag, r.wqkv, r.wout = "f2", inp["ffn_Wqkv"], inp["L0_ffn_Wproj"]
        attention_pass(nc, "ffn", r)
        r.tag = "e2"
        expert_pass(nc, r)
        r.tag = "l"
        last_pass(nc, r)


def laid_out(inputs):
    a = {k: np.asarray(v) for k, v in inputs.items()}
    a["ffn_Wqkv"] = a.pop("L0_ffn_Wqkv").reshape(D, H, 3, HD).transpose(0, 2, 1, 3).reshape(D, 3 * D)
    a["attn_Wqkv"] = np.concatenate([a.pop("L0_attn_Wq"), a.pop("L0_attn_Wk"), a.pop("L0_attn_Wv")], axis=1)
    a["ffn_b1"] = a.pop("L0_ffn_b1").reshape(E, FC, P).transpose(0, 2, 1).reshape(E * P, FC)
    inv_freq = (1.0 / 10000.0 ** (np.arange(0, HD, 2, dtype=np.float32) / HD)).astype(np.float32)
    angle = np.arange(S, dtype=np.float32)[:, None] * inv_freq
    cos, sin = np.cos(angle), np.sin(angle)
    tile = lambda v: v.reshape(T, P, HD).transpose(1, 0, 2).astype(np.float32)
    a["rope_cos"] = tile(np.concatenate([cos, cos], axis=1))
    a["rope_sin"] = tile(np.concatenate([-sin, sin], axis=1))
    return {k: np.ascontiguousarray(v) for k, v in a.items()}


def kernel(**inputs):
    import concourse.bacc as bacc
    from concourse.bass_utils import run_bass_kernel_spmd

    nc = bacc.Bacc("TRN2", target_bir_lowering=False, num_devices=1)
    arrays = laid_out(inputs)
    aps = {k: nc.dram_tensor(f"in_{k}", v.shape, mybir.dt.from_np(v.dtype), kind="ExternalInput").ap()
           for k, v in arrays.items()}
    out = nc.dram_tensor("out", (NB, S, D), F32, kind="ExternalOutput").ap()
    macaron(nc, aps, out)
    result = run_bass_kernel_spmd(nc, [{f"in_{k}": v for k, v in arrays.items()}], core_ids=[0])
    return result.results[0]["out"]
```

```python
from contextlib import ExitStack

import numpy as np

import concourse.bass as bass
from concourse import mybir

F32 = mybir.dt.float32
BF16 = mybir.dt.bfloat16
I32 = mybir.dt.int32
U32 = mybir.dt.uint32
ALU = mybir.AluOpType
ACT = mybir.ActivationFunctionType
AX = mybir.AxisListType

P = 128
D = 128
H = 16
HD = D // H
NB = 32
T = 2
S = T * P
N = NB * S
E = 8
TOPK = 2
CAP = (2 * N + E - 1) // E
F = 4 * D
FC = F // P
GROUP = 4 * P
EPS = 1e-5
SCALE = float(HD) ** -0.5
BIG = 1e30
CLEARS = E * CAP // (8 * P)
JP = H // 2
NQK = 7 * HD
NMAX = 3
DROP = float(1 << 20)

RING = 3
RING_ORDER = [("S0", 1), ("OT", -1), ("ST0", 0), ("S1", 1), ("ST1", 0), ("S2", 1), ("ST2", 0), ("PR", -1),
              ("S3", 1), ("ST3", 0), ("S4", 1), ("ST4", 0), ("S5", 1), ("ST5", 0), ("QT", 2), ("KT", 2),
              ("QKV", 3), ("MT", 1)]
FIRST, LAST = -5, NB + 1
STEADY = (4, NB - 6)

S_UNITS = [(0, 0, 4), (1, 0, 2), (1, 2, 2), (0, 4, 4), (1, 4, 2), (1, 6, 2)]
ST_UNITS = [(0, 0, 2), (0, 2, 2), (1, 0, 4), (0, 4, 2), (0, 6, 2), (1, 4, 4)]


class Seq:

    def __init__(self, reg, const):
        self.reg, self.const, self.par = reg, const, const % 2

    def __add__(self, k):
        return Seq(self.reg, self.const + k)

    def live(self):
        return self.reg is not None or 0 <= self.const < NB

    def count(self, per, extra=0):
        fixed = per * self.const + extra
        return fixed if self.reg is None else self.reg * (2 * per) + fixed

    def of_parity(self, per):
        fixed = per * ((self.const - self.par) // 2 + 1)
        return fixed if self.reg is None else self.reg * per + fixed


def some(value):
    return not isinstance(value, int) or value > 0


def computed(eng, value):
    if not isinstance(value, int):
        eng.compute_val(value)
    return value


def iterations(eng, body):
    for b in range(FIRST, STEADY[0]):
        body(Seq(None, b))
    with eng.Fori(STEADY[0] // 2, STEADY[1] // 2) as i:
        body(Seq(i, 0))
        body(Seq(i, 1))
    for b in range(STEADY[1], LAST + 1):
        body(Seq(None, b))


def new_semaphore(nc, sems, name):
    sems.append(nc.alloc_semaphore(name=name))
    return sems[-1]


def give_back(nc, sems):
    nc.clear_and_free_semaphores(sems)
    nc.all_engine_barrier()


class Ring:

    def __init__(self):
        self.at, n = {}, 0
        self.per = len(RING_ORDER)
        assert self.per % RING == 0
        for b in range(FIRST, LAST + 1):
            for name, ahead in RING_ORDER:
                if 0 <= b + ahead < NB:
                    self.at[name, b + ahead] = n
                    n += 1

    def use(self, name, c):
        ref = c.const if c.reg is None else 8 + c.const
        n = self.at[name, ref]
        fixed = n // RING
        if c.reg is None:
            return n % RING, fixed
        k = self.per // RING
        return n % RING, c.reg * (2 * k) + (fixed - 8 * k)


def attention_pass(nc, kind, r):
    ffn = kind == "ffn"
    ring = Ring()
    sems = []
    with ExitStack() as ctx:
        def sb(name, shape, dt=F32):
            return ctx.enter_context(nc.sbuf_tensor(f"{name}_{r.tag}", shape, dt))

        def sem(name):
            return new_semaphore(nc, sems, f"{name}_{r.tag}")

        psum = ctx.enter_context(nc.psum_tensor(f"psum_{r.tag}", [P, 8, 512], F32))
        o_bank = psum[:, 6, :]
        zt_ps = at_ps = psum[:, 7, 0:S]
        z2_ps = psum[:, 7, S:2 * S]
        logits_ps = psum[:, 7, S:S + T * E].rearrange("p (t e) -> p t e", e=E)
        counts_ps = psum[:, 7, S + 2 * T * E:S + 2 * T * E + (T + 1) * E]

        def slot(n):
            return psum[:, 2 * n:2 * n + 2, :]

        z = sb("z", [P, 2, T, D])
        centered = sb("centered", [P, T, D])
        hT = sb("hT", [P, S])
        qk = sb("qk", [P, 2, T * H, HD])
        vraw = sb("vraw", [P, 2, T, D])
        residual = sb("residual", [P, 2, T * H, HD])
        stack = r.stack
        QT = sb("QT", [P, 2, JP, S], BF16)
        KT = sb("KT", [P, 2, JP, S], BF16)
        mparts = sb("mparts", [P, T, 2, NMAX, JP], BF16)
        mT = sb("mT", [2 * NMAX * JP, S], BF16)
        nmax = sb("nmax", [P, T * H])
        nmax_rest = sb("nmax_rest", [P, T * H])
        V = r.V
        probs0 = sb("probs0", [P, H, S])
        probs1 = sb("probs1", [P, H, P])
        OT = sb("OT", [P, 4, S])
        rden = sb("rden", [P, T, H])
        attn = sb("attn", [P, T, H, HD])
        attnT = sb("attnT", [P, S])
        stats = sb("stats", [P, 3, T, 6])
        mv = sb("mv", [P, 3, T, 2])
        var_eps = sb("var_eps", [P, 3, T])
        rstd = sb("rstd", [P, 3, T])
        again = sb("again", [P, T])
        wqkv = sb("wqkv", [D, 3 * D])
        wout = sb("wout", [D, D])
        if ffn:
            cos = sb("cos", [P, T, HD])
            sin = sb("sin", [P, T, HD])
            swapped = sb("swapped", [P, T, 2 * H, HD])
            g1 = sb("g1", [D, 1])
            b1 = sb("b1", [D, 1])
            g2 = sb("g2", [D, 1])
            b2 = sb("b2", [D, 1])
            wgate = sb("wgate", [D, E])
            z2 = sb("z2", [P, 2, T, D])
            h2T = sb("h2T", [P, S])
            nlmax = sb("nlmax", [P, T])
            lshift = sb("lshift", [P, T, E])
            gexp = sb("gexp", [P, T, E])
            gsum = sb("gsum", [P, T])
            gates = sb("gates", [P, T, E])
            top = sb("top", [P, T, 8])
            top_at = sb("top_at", [P, T, 8], U32)
            expert = sb("expert", [P, T, TOPK])
            onehot = sb("onehot", [P, T, TOPK, E])
            chosen = sb("chosen", [P, T, E], BF16)
            carry = sb("carry", [P, E])
            count = sb("count", [P, T, E])
            picked = sb("picked", [P, T, TOPK, E])
            pos = sb("pos", [P, T * TOPK])
            kept = sb("kept", [P, T * TOPK])
            queue_at = sb("queue_at", [P, T * TOPK])
            over = sb("over", [P, T * TOPK])
            place = sb("place", [P, T * TOPK])
            send_f = sb("send_f", [P, T * TOPK])
            send_to = sb("send_to", [P, 2, T * TOPK], I32)
        else:
            bias = sb("bias", [P, D])
            eo = sb("eo", [P, 2, T * TOPK, D])
            read_at = sb("read_at", [P, 2, T * TOPK], I32)
            moe = sb("moe", [P, T, D])

        loaded = sem("loaded")
        begun = sem("begun")
        sp_begun = sem("sp_begun")
        x_loaded = [sem(f"x_loaded{n}") for n in range(2)]
        drained = [sem(f"drained{n}") for n in range(RING)]
        filled = [sem(f"filled{n}") for n in range(RING)]
        var_ready = {k: sem(f"var_ready{k}") for k in (0, 2)}
        rstd_ready = sem("rstd_ready")
        z_ready = sem("z_ready")
        zt_done = sem("zt_done")
        hT_ready = sem("hT_ready")
        qk_copied = sem("qk_copied")
        rotated = sem("rotated")
        part1_ready = sem("part1_ready")
        rest_ready = sem("rest_ready")
        part2_ready = sem("part2_ready")
        part3_ready = sem("part3_ready")
        QT_ready = sem("QT_ready")
        KT_ready = sem("KT_ready")
        m_ready = sem("m_ready")
        mT_ready = sem("mT_ready")
        max_rows_in = sem("max_rows_in")
        probs_ready = sem("probs_ready")
        V_ready = sem("V_ready")
        pv_done = sem("pv_done")
        OT_ready = sem("OT_ready")
        attn_ready = sem("attn_ready")
        at_done = sem("at_done")
        attnT_ready = sem("attnT_ready")
        if ffn:
            z2_ready = sem("z2_ready")
            h2T_ready = sem("h2T_ready")
            z2t_done = sem("z2t_done")
            logits_done = sem("logits_done")
            logits_read = sem("logits_read")
            counts_done = sem("counts_done")
            counts_read = sem("counts_read")
            pos_ready = sem("pos_ready")
            placed = sem("placed")
            shift_ready = sem("shift_ready")
            gexp_ready = sem("gexp_ready")
            chosen_ready = sem("chosen_ready")
            send_ready = sem("send_ready")
            sent = [sem(f"sent{n}") for n in range(2)]
            cleared = sem("cleared")
        else:
            gathered = [sem(f"gathered{n}") for n in range(2)]
            combined = sem("combined")
            index_ready = sem("index_ready")

        block = ctx.enter_context(nc.Block())

        rows = [slice(64 * a, 64 * a + NQK) for a in range(2)]
        rows_m = [slice(64 * a, 64 * a + NQK + NMAX) for a in range(2)]

        @block.sync
        def _(sp):
            sp.sem_inc(sp_begun, 1)
            loads = [(wqkv[:], r.wqkv), (wout[:], r.wout)]
            if ffn:
                loads += [(g1[:], r.ln1_g), (b1[:], r.ln1_b), (g2[:], r.ln2_g), (b2[:], r.ln2_b),
                          (wgate[:], r.wgate), (cos[:], r.cos), (sin[:], r.sin)]
            else:
                loads += [(bias[:], r.bias.to_broadcast([P, D]))]
            for dst, src in loads:
                sp.dma_start(dst, src).then_inc(loaded, 16)

            def load(c):
                if some(due := computed(sp, (c + -2).of_parity(16))):
                    sp.wait_ge(sp_begun, 1)
                    sp.wait_ge(x_loaded[c.par], due)
                sp.dma_start(r.X[:, bass.ds(c.count(S), S)].rearrange("p (t d) -> p t d", t=T),
                             r.x[bass.ds(c.count(S), S), :].rearrange("(t p) d -> p t d", p=P)
                             ).then_inc(x_loaded[c.par], 16)

            def place_max_rows(c):
                due = computed(sp, c.count(1, 1))
                sp.wait_ge(sp_begun, 1)
                sp.wait_ge(mT_ready, due)
                for a in range(2):
                    row, at = 64 * a + NQK, a * NMAX * JP
                    sp.dma_start(QT[row:row + NMAX, c.par, :, :],
                                 mT[at:at + NMAX * JP, :]).then_inc(max_rows_in, 16)

            def clear_slots(n):
                at = bass.ts(n, 8 * P)
                sp.dma_start(r.expert_in[at, :].rearrange("(p c) d -> p c d", c=8), r.zeros[:]
                             ).then_inc(cleared, 16)

            def body(b):
                if r.loads_x and (b + 6).live():
                    load(b + 6)
                if r.loads_x and b.reg is None and b.const < -1:
                    for n in range(b.const - FIRST, CLEARS, -1 - FIRST):
                        clear_slots(n)
                if (b + 1).live():
                    place_max_rows(b + 1)

            if r.loads_x:
                load(Seq(None, 0))
            iterations(sp, body)
            sp.wait_ge(loaded, 16 * len(loads))
        n_loads = 9 if ffn else 3

        @block.tensor
        def _(pe):
            pe.wait_ge(loaded, 16 * n_loads)

            def transposed_values(c):
                pe.wait_ge(OT_ready, c.count(2, 2))
                n, uses = ring.use("OT", c)
                if some(uses):
                    pe.wait_ge(drained[n], uses)
                for t in range(T):
                    for s in range(4):
                        last = nc.tensor.transpose(slot(n)[:, t, s * P:(s + 1) * P],
                                                   OT[:, s, t * P:(t + 1) * P], r.identf[:])
                last.then_inc(filled[n], 1)

            def transpose_z(c):
                pe.wait_ge(z_ready, c.count(1, 1))
                if some(due := c.count(1)):
                    pe.wait_ge(hT_ready, due)
                if some(due := c.count(1, -3)):
                    pe.wait_ge(attnT_ready, due)
                for t in range(T):
                    last = nc.tensor.transpose(zt_ps[:, t * P:(t + 1) * P], z[:, c.par, t, :], r.identf[:])
                last.then_inc(zt_done, 1)

            def qkv(c):
                pe.wait_ge(hT_ready, c.count(1, 1))
                n, uses = ring.use("QKV", c)
                if some(uses):
                    pe.wait_ge(drained[n], uses)
                for t in range(T):
                    last = nc.tensor.matmul(slot(n)[:, t, 0:3 * D], hT[:, t * P:(t + 1) * P], wqkv[:],
                                            start=True, stop=True)
                last.then_inc(filled[n], 1)

            def maxima_unit(u, c):
                t, j0, nj = S_UNITS[u]
                if u == 0:
                    pe.wait_ge(QT_ready, c.count(1, 1))
                    pe.wait_ge(KT_ready, c.count(1, 1))
                n, uses = ring.use(f"S{u}", c)
                if some(uses):
                    pe.wait_ge(drained[n], uses)
                for a in range(2):
                    out = slot(n)[:, a, :].rearrange("p (j k) -> p j k", j=nj)
                    nc.tensor.matmul(out[:, :, t * P:(t + 1) * P], r.identb[:],
                                     r.above[:, None, :].to_broadcast([P, nj, P]), start=True, stop=False,
                                     skip_group_check=True)
                for j in range(nj):
                    for a in range(2):
                        out = slot(n)[:, a, :].rearrange("p (j k) -> p j k", j=nj)
                        last = nc.tensor.matmul(out[:, j, :], QT[rows[a], c.par, j0 + j, t * P:(t + 1) * P],
                                                KT[rows[a], c.par, j0 + j, 0:(t + 1) * P],
                                                start=False, stop=True, skip_group_check=True)
                last.then_inc(filled[n], 1)

            def scores_unit(u, c):
                t, j0, nj = ST_UNITS[u]
                if u == 0:
                    pe.wait_ge(max_rows_in, c.count(32, 32))
                n, uses = ring.use(f"ST{u}", c)
                if some(uses):
                    pe.wait_ge(drained[n], uses)
                for a in range(2):
                    out = slot(n)[:, a, :].rearrange("p (j q) -> p j q", j=nj)
                    nc.tensor.matmul(out[:, :, 0:P], r.identb[:], r.later[:, None, :].to_broadcast([P, nj, P]),
                                     start=True, stop=False, skip_group_check=True)
                for j in range(nj):
                    for a in range(2):
                        out = slot(n)[:, a, :].rearrange("p (j q) -> p j q", j=nj)
                        last = nc.tensor.matmul(out[:, j, :], KT[rows_m[a], c.par, j0 + j, t * P:(t + 1) * P],
                                                QT[rows_m[a], c.par, j0 + j, t * P:S], start=False, stop=True,
                                                skip_group_check=True)
                last.then_inc(filled[n], 1)

            def values(half, s, c):
                if s == 0:
                    pe.wait_ge(probs_ready, c.count(6, 3 * half + 3))
                    if some(due := c.count(2, half)):
                        pe.wait_ge(OT_ready, due)
                    if half == 0:
                        pe.wait_ge(V_ready, c.count(1, 1))
                for t in range(T):
                    for g in range(4):
                        h = 4 * (2 * half + s) + g
                        probs = (probs0 if t == 0 else probs1)[:, h, :]
                        last = nc.tensor.matmul(o_bank[32 * g:32 * g + 32, s * S + t * P:(s + 1) * S],
                                                V[:, c.par, t, h, :], probs, start=(t == 0), stop=(t == 1),
                                                skip_group_check=True)
                if s == 1:
                    last.then_inc(pv_done, 1)

            def transpose_attn(c):
                pe.wait_ge(attn_ready, c.count(1, 1))
                pe.wait_ge(hT_ready, c.count(1, 4) if c.reg is not None else min(c.const + 4, NB))
                if ffn and some(due := c.count(1)):
                    pe.wait_ge(counts_read, due)
                for t in range(T):
                    last = nc.tensor.transpose(at_ps[:, t * P:(t + 1) * P],
                                               attn[:, t].rearrange("p h d -> p (h d)"), r.identf[:])
                last.then_inc(at_done, 1)

            def project(c):
                pe.wait_ge(attnT_ready, c.count(1, 1))
                n, uses = ring.use("PR", c)
                if some(uses):
                    pe.wait_ge(drained[n], uses)
                for t in range(T):
                    last = nc.tensor.matmul(slot(n)[:, 0, t * D:(t + 1) * D], attnT[:, t * P:(t + 1) * P],
                                            wout[:], start=True, stop=True)
                last.then_inc(filled[n], 1)

            def transpose_z2(c):
                pe.wait_ge(z2_ready, c.count(1, 1))
                pe.wait_ge(hT_ready, c.count(1, 5) if c.reg is not None else min(c.const + 5, NB))
                for t in range(T):
                    last = nc.tensor.transpose(z2_ps[:, t * P:(t + 1) * P], z2[:, c.par, t, :], r.identf[:])
                last.then_inc(z2t_done, 1)

            def router(c):
                pe.wait_ge(h2T_ready, c.count(1, 1))
                for t in range(T):
                    last = nc.tensor.matmul(logits_ps[:, t, :], h2T[:, t * P:(t + 1) * P],
                                            wgate[:], start=True, stop=True)
                last.then_inc(logits_done, 1)

            def counts(c):
                pe.wait_ge(chosen_ready, c.count(1, 1))
                out = counts_ps
                nc.tensor.matmul(out[:, 0:E], r.upto[:], chosen[:, 0, :], start=True, stop=True)
                nc.tensor.matmul(out[:, E:2 * E], r.ones[:], chosen[:, 0, :], start=True, stop=False)
                nc.tensor.matmul(out[:, E:2 * E], r.upto[:], chosen[:, 1, :], start=False, stop=True)
                nc.tensor.matmul(out[:, 2 * E:3 * E], r.ones[:], chosen[:, 0, :], start=True, stop=False)
                last = nc.tensor.matmul(out[:, 2 * E:3 * E], r.ones[:], chosen[:, 1, :], start=False, stop=True)
                last.then_inc(counts_done, 1)

            def transpose_stack(name, side, c):
                if name == "QT":
                    pe.wait_ge(part3_ready, c.count(1, 1))
                n, uses = ring.use(name, c)
                if some(uses):
                    pe.wait_ge(drained[n], uses)
                out = slot(n).bitcast(BF16)
                for t in range(T):
                    for j in range(JP):
                        src = stack[:, c.par, side, t * H + 2 * j:t * H + 2 * j + 2, :, :]
                        last = nc.tensor.transpose(out[:, t, j * P:(j + 1) * P],
                                                   src.rearrange("p h s d -> p (h s d)"), r.identb[:])
                last.then_inc(filled[n], 1)

            def transpose_maxima(c):
                due = computed(pe, c.count(1, 1))
                n, uses = ring.use("MT", c)
                uses = computed(pe, uses)
                pe.wait_ge(loaded, 16 * n_loads)
                pe.wait_ge(m_ready, due)
                if some(uses):
                    pe.wait_ge(drained[n], uses)
                out = slot(n).bitcast(BF16)
                for t in range(T):
                    last = nc.tensor.transpose(out[0:2 * NMAX * JP, 0, t * P:(t + 1) * P],
                                               mparts[:, t].rearrange("p a k j -> p (a k j)"), r.identb[:])
                last.then_inc(filled[n], 1)

            def body(b):
                for u in range(6):
                    if (b + 1).live():
                        maxima_unit(u, b + 1)
                    if u == 0 and ffn and (b + -2).live():
                        counts(b + -2)
                    if u == 0 and (b + -1).live():
                        transposed_values(b + -1)
                    if b.live():
                        scores_unit(u, b)
                    if u == 1 and (b + -1).live():
                        transpose_attn(b + -1)
                    if u == 2 and (b + -1).live():
                        project(b + -1)
                    if u in (3, 4) and b.live():
                        values(0, u - 3, b)
                    if u == 3 and (b + 3).live():
                        transpose_z(b + 3)
                    if u == 4 and ffn and (b + -1).live():
                        transpose_z2(b + -1)
                    if u == 5 and ffn and (b + -1).live():
                        router(b + -1)
                if (b + 2).live():
                    transpose_stack("QT", 0, b + 2)
                    transpose_stack("KT", 1, b + 2)
                if (b + 3).live():
                    qkv(b + 3)
                if (b + 1).live():
                    transpose_maxima(b + 1)
                if b.live():
                    values(1, 0, b)
                    values(1, 1, b)

            iterations(pe, body)

        @block.scalar
        def _(act):
            act.wait_ge(loaded, 16 * n_loads)

            def copy_hT(c):
                act.wait_ge(zt_done, c.count(1, 1))
                if ffn:
                    nc.scalar.activation(hT[:], zt_ps, ACT.Identity, scale=g1[:], bias=b1[:]).then_inc(hT_ready, 1)
                else:
                    nc.scalar.activation(hT[:], zt_ps, ACT.Copy).then_inc(hT_ready, 1)

            def copy_qkv(c):
                n, uses = ring.use("QKV", c)
                act.wait_ge(filled[n], uses + 1)
                if some(due := c.count(1)):
                    act.wait_ge(rest_ready, due)
                if some(due := c.count(1, -1)):
                    act.wait_ge(V_ready, due)
                nc.scalar.activation(qk[:].rearrange("p k (t h) d -> p t k (h d)", t=T),
                                     slot(n)[:, :, 0:2 * D].rearrange("p t (k n) -> p t k n", k=2),
                                     ACT.Copy).then_inc(qk_copied, 1)
                nc.scalar.activation(vraw[:, c.par], slot(n)[:, :, 2 * D:3 * D], ACT.Copy).then_inc(drained[n], 1)

            def exponentials(u, c):
                t, j0, nj = ST_UNITS[u]
                n, uses = ring.use(f"ST{u}", c)
                act.wait_ge(filled[n], uses + 1)
                if some(due := c.count(2, -1 + u // 3)):
                    act.wait_ge(pv_done, due)
                dst = (probs0 if t == 0 else probs1)[:, 2 * j0:2 * (j0 + nj), :].rearrange("p (j a) q -> p a j q", a=2)
                nc.scalar.activation(dst, slot(n).rearrange("p a (j q) -> p a j q", j=nj), ACT.Exp,
                                     scale=SCALE).then_inc(drained[n], 1)
                act.drain().then_inc(probs_ready, 1)

            def first_part(c):
                act.wait_ge(rotated if ffn else qk_copied, c.count(1, 1))
                nc.scalar.activation(stack[:, c.par, 0, :, 0:3, :],
                                     qk[:, 0, :, None, :].to_broadcast([P, T * H, 3, HD]), ACT.Copy)
                nc.scalar.activation(stack[:, c.par, 1, :, 0:7:3, :],
                                     qk[:, 1, :, None, :].to_broadcast([P, T * H, 3, HD]),
                                     ACT.Copy).then_inc(part1_ready, 1)

            def second_part(c):
                act.wait_ge(rest_ready, c.count(1, 1))
                nc.scalar.activation(stack[:, c.par, 0, :, 3:6, :],
                                     residual[:, 0, :, None, :].to_broadcast([P, T * H, 3, HD]), ACT.Copy)
                nc.scalar.activation(stack[:, c.par, 1, :, 1:5:3, :],
                                     residual[:, 1, :, None, :].to_broadcast([P, T * H, 2, HD]),
                                     ACT.Copy).then_inc(part2_ready, 1)

            def copy_attnT(c):
                act.wait_ge(at_done, c.count(1, 1))
                if (c + -1).live():
                    k, uses = ring.use("PR", c + -1)
                    act.wait_ge(filled[k], uses + 1)
                nc.scalar.activation(attnT[:], at_ps, ACT.Copy).then_inc(attnT_ready, 1)

            def copy_values(half, c):
                act.wait_ge(pv_done, c.count(2, half + 1))
                if half == 0 and (c + -1).live():
                    k, uses = ring.use("OT", c + -1)
                    act.wait_ge(filled[k], uses + 1)
                nc.scalar.activation(OT[:, 2 * half:2 * half + 2, :].rearrange("p s q -> p (s q)"), o_bank,
                                     ACT.Copy).then_inc(OT_ready, 1)

            def copy_h2T(c):
                act.wait_ge(z2t_done, c.count(1, 1))
                if some(due := c.count(1)):
                    act.wait_ge(logits_done, due)
                nc.scalar.activation(h2T[:], z2_ps, ACT.Identity, scale=g2[:], bias=b2[:]).then_inc(h2T_ready, 1)

            def gate_exp(c):
                act.wait_ge(shift_ready, c.count(1, 1))
                nc.scalar.activation(gexp[:], lshift[:], ACT.Exp).then_inc(gexp_ready, 1)

            def copy_stack(name, dst, done, c):
                n, uses = ring.use(name, c)
                act.wait_ge(filled[n], uses + 1)
                nc.scalar.activation(dst.rearrange("p j (t q) -> p t j q", t=T),
                                     slot(n).bitcast(BF16).rearrange("p t (j q) -> p t j q", j=JP),
                                     ACT.Copy).then_inc(done, 1)
                act.drain().then_inc(drained[n], 1)

            def place_V(c):
                if some(due := c.count(2, -2)):
                    act.wait_ge(pv_done, due)
                nc.scalar.activation(V[:, c.par, :, :, 0:HD], vraw[:, c.par].rearrange("p t (h d) -> p t h d", d=HD),
                                     ACT.Copy).then_inc(V_ready, 1)

            def body(b):
                if b.live():
                    exponentials(0, b)
                    exponentials(1, b)
                if (b + -1).live():
                    copy_attnT(b + -1)
                if (b + 2).live():
                    first_part(b + 2)
                if b.live():
                    exponentials(2, b)
                    exponentials(3, b)
                if (b + 2).live():
                    second_part(b + 2)
                if (b + 3).live():
                    copy_hT(b + 3)
                if b.live():
                    exponentials(4, b)
                    copy_values(0, b)
                if ffn and (b + -1).live():
                    copy_h2T(b + -1)
                if b.live():
                    exponentials(5, b)
                if ffn and (b + -1).live():
                    gate_exp(b + -1)
                if (b + 2).live():
                    copy_stack("QT", QT[:, (b + 2).par], QT_ready, b + 2)
                    copy_stack("KT", KT[:, (b + 2).par], KT_ready, b + 2)
                if (b + 3).live():
                    copy_qkv(b + 3)
                if b.live():
                    copy_values(1, b)
                if (b + 2).live():
                    place_V(b + 2)

            iterations(act, body)

        @block.vector
        def _(dve):
            if ffn:
                nc.vector.memset(carry[:], 0.0)
                dve.drain()
            dve.wait_ge(loaded, 16 * n_loads)

            def tokens(buf, c, t):
                return buf[:, bass.ds(c.count(S, t * D), D)]

            def ln_stats(k, src):
                for t in range(T):
                    nc.vector.bn_stats(stats[:, k, t, :], src(t))
                dve.drain()
                for t in range(T):
                    nc.vector.bn_aggr(mv[:, k, t, :], stats[:, k, t, :])
                dve.drain()
                nc.vector.tensor_scalar(var_eps[:, k, :], mv[:, k, :, 1], EPS, None,
                                        ALU.add).then_inc(var_ready[k], 1)

            def apply_router_norm(c):
                dve.wait_ge(rstd_ready, c.count(1, 1))
                if some(due := (c + -2).of_parity(16 * T * TOPK)):
                    dve.wait_ge(sent[c.par], due)
                for t in range(T):
                    last = nc.vector.tensor_scalar(z2[:, c.par, t, :], tokens(r.Y, c, t), mv[:, 2, t, 0:1],
                                                   rstd[:, 2, t:t + 1], ALU.subtract, ALU.mult)
                last.then_inc(z2_ready, 1)

            def combine(c):
                dve.wait_ge(gathered[c.par], c.of_parity(16 * T * TOPK))
                for k in range(TOPK):
                    for t in range(T):
                        n = t * TOPK + k
                        nc.vector.scalar_tensor_tensor(moe[:, t, :], eo[:, c.par, n, :],
                                                       r.gate[:, bass.ds(c.count(T * TOPK, n), 1)],
                                                       tokens(r.Y, c, t) if k == 0 else moe[:, t, :],
                                                       ALU.mult, ALU.add)
                    dve.drain()
                for t in range(T):
                    last = nc.vector.scalar_tensor_tensor(tokens(r.X, c, t), moe[:, t, :], 0.5, tokens(r.X, c, t),
                                                          ALU.mult, ALU.add)
                last.then_inc(combined, 1)
                dve.drain()

            def norm_values(c):
                dve.drain()
                n, uses = ring.use("OT", c)
                dve.wait_ge(filled[n], uses + 1)
                src = slot(n).rearrange("p t (h r) -> p t h r", r=32)
                nc.vector.reciprocal(rden[:], src[:, :, :, HD])
                dve.drain()
                if some(due := c.count(1)):
                    dve.wait_ge(at_done, due)
                for t in range(T):
                    last = nc.vector.tensor_tensor(attn[:, t], src[:, t, :, 0:HD],
                                                   rden[:, t, :, None].to_broadcast([P, H, HD]), ALU.mult)
                last.then_inc(attn_ready, 1)
                dve.drain().then_inc(drained[n], 1)

            def maxima(u, c):
                t, j0, nj = S_UNITS[u]
                n, uses = ring.use(f"S{u}", c)
                dve.wait_ge(filled[n], uses + 1)
                dst = nmax[:, t * H:(t + 1) * H].rearrange("p (j a) -> p a j", a=2)[:, :, j0:j0 + nj]
                nc.vector.tensor_reduce(dst, slot(n).rearrange("p a (j k) -> p a j k", j=nj), AX.X, ALU.max,
                                        negate=True).then_inc(drained[n], 1)

            def maxima_parts(c):
                m = [mparts[:, :, :, k, :] for k in range(NMAX)]
                whole = nmax[:].rearrange("p (t j a) -> p t a j", t=T, a=2)
                left = nmax_rest[:].rearrange("p (t j a) -> p t a j", t=T, a=2)
                dve.drain()
                nc.vector.tensor_copy(m[0], whole)
                dve.drain()
                nc.vector.tensor_tensor(left, whole, m[0], ALU.subtract)
                dve.drain()
                nc.vector.tensor_copy(m[1], left)
                dve.drain()
                nc.vector.tensor_tensor(m[2], left, m[1], ALU.subtract).then_inc(m_ready, 1)

            def rest(c):
                dve.wait_ge(part1_ready, c.count(1, 1))
                nc.vector.tensor_tensor(residual[:].rearrange("p k h d -> p (k h) d"),
                                        qk[:].rearrange("p k h d -> p (k h) d"),
                                        stack[:, c.par].rearrange("p k h s d -> p (k h) s d")[:, :, 0, :],
                                        ALU.subtract).then_inc(rest_ready, 1)

            def third_part(c):
                dve.wait_ge(part2_ready, c.count(1, 1))
                nc.vector.tensor_tensor(stack[:, c.par, 0, :, 6, :], residual[:, 0],
                                        stack[:, c.par, 0, :, 4, :], ALU.subtract)
                nc.vector.tensor_tensor(stack[:, c.par, 1, :, 2:6:3, :],
                                        residual[:, 1, :, None, :].to_broadcast([P, T * H, 2, HD]),
                                        stack[:, c.par, 1, :, 4:5, :].to_broadcast([P, T * H, 2, HD]),
                                        ALU.subtract).then_inc(part3_ready, 1)

            def copy_mT(c):
                n, uses = ring.use("MT", c)
                dve.wait_ge(filled[n], uses + 1)
                if some(due := c.count(32)):
                    dve.wait_ge(max_rows_in, due)
                nc.vector.tensor_copy(mT[:], slot(n).bitcast(BF16)[0:2 * NMAX * JP, 0, 0:S]).then_inc(mT_ready, 1)
                dve.drain().then_inc(drained[n], 1)

            def residual_sum(c):
                n, uses = ring.use("PR", c)
                dve.wait_ge(filled[n], uses + 1)
                out = r.Y if ffn else r.X
                for t in range(T):
                    last = nc.vector.tensor_tensor(tokens(out, c, t), tokens(out, c, t),
                                                   slot(n)[:, 0, t * D:(t + 1) * D], ALU.add)
                last.then_inc(drained[n], 1)
                dve.drain()
                if not ffn:
                    for t in range(T):
                        nc.vector.tensor_tensor(tokens(out, c, t), tokens(out, c, t), bias[:], ALU.add)

            def route_shift(c):
                dve.wait_ge(logits_done, c.count(1, 1))
                nc.vector.tensor_reduce(nlmax[:], logits_ps, AX.X, ALU.max, negate=True)
                dve.drain()
                nc.vector.tensor_tensor(lshift[:], logits_ps, nlmax[:, :, None].to_broadcast([P, T, E]),
                                        ALU.add).then_inc(shift_ready, 1)
                dve.drain().then_inc(logits_read, 1)

            def route_choose(c):
                dve.wait_ge(gexp_ready, c.count(1, 1))
                nc.vector.tensor_reduce(gsum[:], gexp[:], AX.X, ALU.add)
                dve.drain()
                nc.vector.reciprocal(gsum[:], gsum[:])
                dve.drain()
                nc.vector.tensor_tensor(gates[:], gexp[:], gsum[:, :, None].to_broadcast([P, T, E]), ALU.mult)
                dve.drain()
                if some(due := computed(dve, c.count(1))):
                    dve.wait_ge(loaded, 16 * n_loads)
                    dve.wait_ge(placed, due)
                for t in range(T):
                    nc.vector.max(top[:, t, :], gates[:, t, :])
                dve.drain()
                for t in range(T):
                    nc.vector.max_index(top_at[:, t, :], top[:, t, :], gates[:, t, :])
                dve.drain()
                nc.vector.tensor_copy(expert[:], top_at[:, :, 0:TOPK])
                nc.vector.tensor_scalar(queue_at[:].rearrange("p (t k) -> p t k", t=T), top_at[:, :, 0:TOPK],
                                        float(CAP), -1.0, ALU.mult, ALU.add)
                dve.drain()
                nc.vector.tensor_tensor(onehot[:].rearrange("p t k e -> p (t k) e"),
                                        r.iota8[:, None, :].to_broadcast([P, T * TOPK, E]),
                                        expert[:].rearrange("p t k -> p (t k)")[:, :, None]
                                        .to_broadcast([P, T * TOPK, E]), ALU.is_equal)
                dve.drain()
                nc.vector.tensor_tensor(chosen[:], onehot[:, :, 0, :], onehot[:, :, 1, :],
                                        ALU.add).then_inc(chosen_ready, 1)

            def route_queue(c):
                dve.wait_ge(counts_done, c.count(1, 1))
                nc.vector.tensor_tensor(count[:], counts_ps[:, 0:T * E].rearrange("p (t e) -> p t e", e=E),
                                        carry[:, None, :].to_broadcast([P, T, E]), ALU.add)
                dve.drain()
                nc.vector.tensor_tensor(carry[:], counts_ps[:, T * E:(T + 1) * E], carry[:],
                                        ALU.add).then_inc(counts_read, 1)
                nc.vector.tensor_tensor(picked[:], onehot[:],
                                        count[:, :, None, :].to_broadcast([P, T, TOPK, E]), ALU.mult)
                dve.drain()
                if some(due := computed(dve, c.count(1))):
                    dve.wait_ge(loaded, 16 * n_loads)
                    dve.wait_ge(placed, due)
                nc.vector.tensor_reduce(pos[:].rearrange("p (t k) -> p t k", t=T), picked[:], AX.X,
                                        ALU.add).then_inc(pos_ready, 1)

            def body(b):
                if (b + 1).live():
                    maxima(0, b + 1)
                if (b + -1).live():
                    norm_values(b + -1)
                if ffn and (b + -2).live():
                    route_queue(b + -2)
                if (b + 1).live():
                    maxima(1, b + 1)
                    maxima(2, b + 1)
                if (b + -1).live():
                    residual_sum(b + -1)
                    if ffn:
                        ln_stats(2, lambda t: tokens(r.Y, b + -1, t))
                if (b + 2).live():
                    rest(b + 2)
                if (b + 1).live():
                    maxima(3, b + 1)
                    maxima(4, b + 1)
                if ffn and (b + -1).live():
                    apply_router_norm(b + -1)
                if (b + 2).live():
                    third_part(b + 2)
                if (b + 1).live():
                    maxima(5, b + 1)
                if ffn and (b + -1).live():
                    route_shift(b + -1)
                if (b + 4).live():
                    if not ffn:
                        combine(b + 4)
                    dve.drain()
                    if r.loads_x:
                        dve.wait_ge(x_loaded[(b + 4).par], (b + 4).of_parity(16))
                    if some(due := computed(dve, (b + 4).count(1))):
                        dve.wait_ge(loaded, 16 * n_loads)
                        dve.wait_ge(z_ready, due)
                    ln_stats(0, lambda t: tokens(r.X, b + 4, t))
                if (b + 1).live():
                    maxima_parts(b + 1)
                if (b + 1).live():
                    copy_mT(b + 1)
                if ffn and (b + -1).live():
                    route_choose(b + -1)
            iterations(dve, body)

        @block.gpsimd
        def _(pool):
            pool.sem_inc(begun, 1)
            last_slot = pool.to_reg(E * CAP - 1)

            def root(k, c):
                pool.wait_ge(var_ready[k], c.count(1, 1))
                done = nc.gpsimd.tensor_tensor(rstd[:, k, :], var_eps[:, k, :], r.minus_half[:, 0:T], ALU.pow)
                if k == 2:
                    done.then_inc(rstd_ready, 1)

            def root_again(c):
                first, second, v = rstd[:, 0, :], rstd[:, 1, :], again[:]
                pool.drain()
                nc.gpsimd.tensor_tensor(v, mv[:, 0, :, 1], first, ALU.mult)
                pool.drain()
                nc.gpsimd.tensor_tensor(v, v, first, ALU.mult)
                pool.drain()
                nc.gpsimd.tensor_scalar(v, v, EPS, None, ALU.add)
                pool.drain()
                nc.gpsimd.tensor_tensor(v, v, r.minus_half[:, 0:T], ALU.pow)
                pool.drain()
                nc.gpsimd.tensor_tensor(second, v, first, ALU.mult)

            def apply_norm(c):
                pool.drain()
                if some(due := computed(pool, c.count(1, -1))):
                    pool.wait_ge(begun, 1)
                    pool.wait_ge(zt_done, due)
                here = bass.ds(c.count(S), S)

                def scale(k):
                    return rstd[:, k, :, None].to_broadcast([P, T, D])

                nc.gpsimd.tensor_tensor(centered[:], r.X[:, here].rearrange("p (t d) -> p t d", t=T),
                                        mv[:, 0, :, 0:1].to_broadcast([P, T, D]), ALU.subtract)
                pool.drain()
                if ffn:
                    nc.gpsimd.tensor_tensor(r.Y[:, here].rearrange("p (t d) -> p t d", t=T), centered[:],
                                            scale(0), ALU.mult)
                last = nc.gpsimd.tensor_tensor(z[:, c.par], centered[:], scale(1 if ffn else 0), ALU.mult)
                last.then_inc(z_ready, 1)

            def rotate(c):
                pool.wait_ge(qk_copied, c.count(1, 1))
                for k in range(2):
                    for t in range(T):
                        src = qk[:, k, t * H:(t + 1) * H, :]
                        nc.gpsimd.tensor_tensor(swapped[:, t, k * H:(k + 1) * H, :]
                                                .rearrange("p h (u e) -> p h u e", u=2),
                                                src.rearrange("p h (u e) -> p h u e", u=2)[:, :, ::-1, :],
                                                sin[:, t, None, :].to_broadcast([P, H, HD])
                                                .rearrange("p h (u e) -> p h u e", u=2), ALU.mult)
                pool.drain()
                for k in range(2):
                    for t in range(T):
                        src = qk[:, k, t * H:(t + 1) * H, :]
                        nc.gpsimd.tensor_tensor(src, src, cos[:, t, None, :].to_broadcast([P, H, HD]), ALU.mult)
                pool.drain()
                for k in range(2):
                    for t in range(T):
                        src = qk[:, k, t * H:(t + 1) * H, :]
                        last = nc.gpsimd.tensor_tensor(src, src, swapped[:, t, k * H:(k + 1) * H, :], ALU.add)
                last.then_inc(rotated, 1)

            def route_place(c):
                due = computed(pool, c.count(1, 1))
                pool.wait_ge(begun, 1)
                pool.wait_ge(pos_ready, due)
                nc.gpsimd.tensor_scalar(over[:], pos[:], CAP + 0.5, DROP, ALU.is_gt, ALU.mult)
                nc.gpsimd.tensor_scalar(kept[:], pos[:], CAP + 0.5, None, ALU.is_le)
                nc.gpsimd.tensor_scalar(place[:], pos[:], float(CAP), None, ALU.min)
                pool.drain()
                nc.gpsimd.tensor_tensor(place[:], place[:], queue_at[:], ALU.add)
                gate_at = bass.ds(c.count(T * TOPK), T * TOPK)
                nc.gpsimd.tensor_tensor(r.gate[:, gate_at].rearrange("p (t k) -> p t k", t=T),
                                        kept[:].rearrange("p (t k) -> p t k", t=T), top[:, :, 0:TOPK], ALU.mult)
                pool.drain()
                nc.gpsimd.tensor_tensor(send_f[:], place[:], over[:], ALU.add).then_inc(placed, 1)
                nc.gpsimd.tensor_copy(r.slots[:, gate_at], place[:])
                pool.drain()
                if some(due := computed(pool, (c + -2).of_parity(16 * T * TOPK))):
                    pool.wait_ge(begun, 1)
                    pool.wait_ge(sent[c.par], due)
                nc.gpsimd.tensor_copy(send_to[:, c.par, :], send_f[:]).then_inc(send_ready, 1)

            def send(c):
                if r.loads_x and c.reg is None and c.const == 0:
                    pool.wait_ge(cleared, 16 * CLEARS)
                due = computed(pool, c.count(1, 1))
                pool.wait_ge(begun, 1)
                pool.wait_ge(send_ready, due)
                for t in range(T):
                    for k in range(TOPK):
                        n = t * TOPK + k
                        nc.gpsimd.indirect_dma_start(
                            out=r.expert_in, out_offset=bass.IndirectOffsetOnAxis(send_to[:, c.par, n:n + 1], 0),
                            in_=z2[:, c.par, t, :], in_offset=None, bounds_check=last_slot,
                            oob_is_err=False).then_inc(sent[c.par], 16)

            def gather(c):
                if some(due := computed(pool, c.count(1, -1))):
                    pool.wait_ge(begun, 1)
                    pool.wait_ge(combined, due)
                if some(due := (c + -2).of_parity(16 * T * TOPK)):
                    pool.wait_ge(gathered[c.par], due)
                nc.gpsimd.tensor_copy(read_at[:, c.par, :],
                                      r.slots[:, bass.ds(c.count(T * TOPK), T * TOPK)]).then_inc(index_ready, 1)
                due = computed(pool, c.count(1, 1))
                pool.wait_ge(begun, 1)
                pool.wait_ge(index_ready, due)
                for n in range(T * TOPK):
                    nc.gpsimd.indirect_dma_start(
                        out=eo[:, c.par, n, :], out_offset=None, in_=r.expert_out,
                        in_offset=bass.IndirectOffsetOnAxis(read_at[:, c.par, n:n + 1], 0),
                        bounds_check=last_slot, oob_is_err=False).then_inc(gathered[c.par], 16)

            def body(b):
                if not ffn and (b + 5).live():
                    gather(b + 5)
                if ffn and (b + -2).live():
                    route_place(b + -2)
                if ffn and (b + -1).live():
                    root(2, b + -1)
                if ffn and (b + -2).live():
                    send(b + -2)
                if (b + 4).live():
                    root(0, b + 4)
                    if ffn:
                        root_again(b + 4)
                if ffn and (b + 3).live():
                    rotate(b + 3)
                if (b + 4).live():
                    apply_norm(b + 4)

            iterations(pool, body)
            if ffn:
                for par in range(2):
                    pool.wait_ge(sent[par], 16 * T * TOPK * NB // 2)
    give_back(nc, sems)



def expert_pass(nc, r):
    per_expert = CAP // GROUP
    groups = 2 * per_expert
    pairs = E // 2
    sems = []
    with ExitStack() as ctx:
        def sb(name, shape, dt=F32):
            return ctx.enter_context(nc.sbuf_tensor(f"{name}_{r.tag}", shape, dt))

        def sem(name):
            return new_semaphore(nc, sems, f"{name}_{r.tag}")

        psum = ctx.enter_context(nc.psum_tensor(f"psum_{r.tag}", [P, 8, 512], F32))
        xt_ps, back_ps = psum[:, 0, :], psum[:, 1, :]

        def hidden_ps(k):
            return psum[:, 2 + k % 4, :]

        def out_ps(n):
            return psum[:, 6 + n % 2, :]

        w1 = sb("w1", [D, 2, F])
        w2 = sb("w2", [P, 2, FC, D])
        bias1 = sb("bias1", [P, 2, FC])
        bias2 = sb("bias2", [D, 2])
        gain = sb("gain", [D, 1])
        shift = sb("shift", [D, 1])
        rows = sb("rows", [P, 2, 4, D])
        xT = sb("xT", [D, 2, GROUP])
        hidden = sb("hidden", [P, 2, FC, GROUP])
        outT = sb("outT", [D, GROUP])
        back = sb("back", [P, 2, 4, D])

        loaded = sem("loaded")
        weights = [sem(f"weights{n}") for n in range(2)]
        rows_in = [sem(f"rows_in{n}") for n in range(2)]
        xt_done = sem("xt_done")
        xT_ready = sem("xT_ready")
        hidden_done = sem("hidden_done")
        gelu_ready = sem("gelu_ready")
        out_done = sem("out_done")
        outT_ready = sem("outT_ready")
        back_done = sem("back_done")
        back_ready = sem("back_ready")
        stored = [sem(f"stored{n}") for n in range(2)]
        sp_begun = sem("sp_begun")
        block = ctx.enter_context(nc.Block())

        class Group:

            def __init__(self, reg, const):
                self.reg, self.const, self.par = reg, const, const % 2

            def count(self, per, extra=0):
                fixed = per * self.const + extra
                return fixed if self.reg is None else self.reg * (groups * per) + fixed

            def of_parity(self, per):
                fixed = per * ((self.const - self.par) // 2 + 1)
                return fixed if self.reg is None else self.reg * (groups // 2 * per) + fixed

        total = pairs * groups

        def all_groups(eng, body):
            for g in range(-1, groups):
                body(Group(None, g), g >= 0, True)
            with eng.Fori(1, pairs - 1) as i:
                for g in range(groups):
                    body(Group(i, g), True, True)
            for g in range(total - groups, total + 1):
                body(Group(None, g), g < total, g + 1 < total)

        @block.sync
        def _(sp):
            sp.sem_inc(sp_begun, 1)
            sp.dma_start(gain[:], r.ln2_g).then_inc(loaded, 16)
            sp.dma_start(shift[:], r.ln2_b).then_inc(loaded, 16)

            def fetch(g):
                if some(due := computed(sp, g.count(1, -1))):
                    sp.wait_ge(sp_begun, 1)
                    sp.wait_ge(xt_done, due)
                if some(due := g.of_parity(16) - 16):
                    sp.wait_ge(rows_in[g.par], due)
                sp.dma_start(rows[:, g.par], r.expert_in[bass.ds(g.count(GROUP), GROUP), :]
                             .rearrange("(p c) d -> p c d", c=4)).then_inc(rows_in[g.par], 16)

            def fetch_weights(e, experts_before):
                at = e % 2
                n = experts_before
                if some(due := computed(sp, n * per_expert - per_expert)):
                    sp.wait_ge(sp_begun, 1)
                    sp.wait_ge(out_done, due)
                sp.dma_start(w1[:, at], r.w1[bass.ds(n * D, D), :]).then_inc(weights[at], 16)
                sp.dma_start(w2[:, at], r.w2[bass.ds(n * F, F), :].rearrange("(c p) d -> p c d", p=P)
                             ).then_inc(weights[at], 16)
                sp.dma_start(bias1[:, at], r.bias1[bass.ds(n * P, P), :]).then_inc(weights[at], 16)
                sp.dma_start(bias2[:, at:at + 1], r.bias2[bass.ds(n * D, D), :]).then_inc(weights[at], 16)

            def store(g):
                due = computed(sp, g.count(1, 1))
                sp.wait_ge(sp_begun, 1)
                sp.wait_ge(back_ready, due)
                sp.dma_start(r.expert_out[bass.ds(g.count(GROUP), GROUP), :].rearrange("(p c) d -> p c d", c=4),
                             back[:, g.par]).then_inc(stored[g.par], 16)

            def step(g, ahead):
                if ahead:
                    fetch(Group(g.reg, g.const + 2))
                store(g)

            fetch_weights(0, 0)
            fetch(Group(None, 0))
            fetch(Group(None, 1))
            fetch_weights(1, 1)
            for g in range(groups):
                step(Group(None, g), True)
                if g % per_expert == per_expert - 1:
                    fetch_weights(g // per_expert, g // per_expert + 2)
            with sp.Fori(1, pairs - 1) as i:
                for g in range(groups):
                    step(Group(i, g), True)
                    if g % per_expert == per_expert - 1:
                        fetch_weights(g // per_expert, i * 2 + (g // per_expert + 2))
            for g in range(total - groups, total):
                step(Group(None, g), g + 2 < total)
            for par in range(2):
                sp.wait_ge(stored[par], 16 * total // 2)

        def weights_count(g):
            return 64 * (g.const // groups + 1) if g.reg is None else g.reg * 64 + 64

        @block.tensor
        def _(pe):
            def transpose_in(g):
                pe.wait_ge(rows_in[g.par], g.of_parity(16))
                if some(due := g.count(1)):
                    pe.wait_ge(xT_ready, due)
                for c in range(4):
                    last = nc.tensor.transpose(xt_ps[:, c * P:(c + 1) * P], rows[:, g.par, c, :], r.identf[:])
                last.then_inc(xt_done, 1)

            def first_matrix(g, f):
                if f == 0:
                    if g.const % per_expert == 0:
                        pe.wait_ge(weights[g.const // per_expert % 2], weights_count(g))
                    pe.wait_ge(xT_ready, g.count(1, 1))
                if some(due := g.count(4, f + 1 - 4)):
                    pe.wait_ge(gelu_ready, due)
                at = g.const // per_expert % 2
                nc.tensor.matmul(hidden_ps(f), w1[:, at, f * P:(f + 1) * P], xT[:, g.par, :],
                                 start=True, stop=True).then_inc(hidden_done, 1)

            def second_matrix(g):
                if some(due := g.count(1, -1)):
                    pe.wait_ge(outT_ready, due)
                at = g.const // per_expert % 2
                for f in range(FC):
                    pe.wait_ge(gelu_ready, g.count(4, f + 1))
                    last = nc.tensor.matmul(out_ps(g.par), w2[:, at, f, :], hidden[:, g.par, f, :],
                                            start=(f == 0), stop=(f == FC - 1))
                last.then_inc(out_done, 1)

            def transpose_back(g):
                pe.wait_ge(outT_ready, g.count(1, 1))
                if some(due := g.count(1)):
                    pe.wait_ge(back_ready, due)
                for c in range(4):
                    last = nc.tensor.transpose(back_ps[:, c * P:(c + 1) * P], outT[:, c * P:(c + 1) * P],
                                               r.identf[:])
                last.then_inc(back_done, 1)

            def body(g, now, ahead):
                before = Group(g.reg, g.const - 1)
                behind = now and (g.reg is not None or g.const > 0) or not now and g.const == total
                if now:
                    first_matrix(g, 0)
                    first_matrix(g, 1)
                if behind:
                    transpose_back(before)
                if now:
                    first_matrix(g, 2)
                    first_matrix(g, 3)
                if ahead:
                    transpose_in(Group(g.reg, g.const + 1))
                if now:
                    second_matrix(g)

            all_groups(pe, body)

        @block.scalar
        def _(act):
            def body(g, now, ahead):
                if not now:
                    return
                at = g.const // per_expert % 2
                if g.const % per_expert == 0:
                    act.wait_ge(weights[g.const // per_expert % 2], weights_count(g))
                for f in range(FC):
                    act.wait_ge(hidden_done, g.count(4, f + 1))
                    if f == 0:
                        if some(due := g.count(1, -1)):
                            act.wait_ge(out_done, due)
                    nc.scalar.activation(hidden[:, g.par, f, :], hidden_ps(f), ACT.Gelu,
                                         bias=bias1[:, at, f:f + 1]).then_inc(gelu_ready, 1)

            all_groups(act, body)

        @block.vector
        def _(dve):
            dve.wait_ge(loaded, 32)

            def copy_in(g):
                dve.wait_ge(xt_done, g.count(1, 1))
                if some(due := g.count(4, -4)):
                    dve.wait_ge(hidden_done, due)
                nc.vector.tensor_scalar(xT[:, g.par, :], xt_ps, gain[:], shift[:], ALU.mult,
                                        ALU.add).then_inc(xT_ready, 1)

            def copy_out(g):
                dve.wait_ge(out_done, g.count(1, 1))
                if some(due := g.count(1)):
                    dve.wait_ge(back_done, due)
                at = g.const // per_expert % 2
                if g.const % per_expert == 0:
                    dve.wait_ge(weights[g.const // per_expert % 2], weights_count(g))
                nc.vector.tensor_scalar(outT[:], out_ps(g.par), bias2[:, at:at + 1], None,
                                        ALU.add).then_inc(outT_ready, 1)

            def copy_back(g):
                dve.wait_ge(back_done, g.count(1, 1))
                if some(due := Group(g.reg, g.const - 2).of_parity(16)):
                    dve.wait_ge(stored[g.par], due)
                nc.vector.tensor_copy(back[:, g.par].rearrange("p c d -> p (c d)"), back_ps).then_inc(back_ready, 1)

            def body(g, now, ahead):
                before = Group(g.reg, g.const - 1)
                behind = now and (g.reg is not None or g.const > 0) or not now and g.const == total
                if behind:
                    copy_back(before)
                if ahead:
                    copy_in(Group(g.reg, g.const + 1))
                if now:
                    copy_out(g)

            all_groups(dve, body)
    give_back(nc, sems)


def last_pass(nc, r):
    sems = []
    with ExitStack() as ctx:
        def sb(name, shape, dt=F32):
            return ctx.enter_context(nc.sbuf_tensor(f"{name}_{r.tag}", shape, dt))

        def sem(name):
            return new_semaphore(nc, sems, f"{name}_{r.tag}")

        K = T * TOPK
        eo = sb("eo", [P, 2, K, D])
        read_at = sb("read_at", [P, 2, K], I32)
        moe = sb("moe", [P, T, D])
        result = sb("result", [P, 2, T, D])
        index_ready = sem("index_ready")
        gathered = [sem(f"gathered{n}") for n in range(2)]
        combined = sem("combined")
        begun = sem("begun")
        sp_begun = sem("sp_begun")
        stored = [sem(f"stored{n}") for n in range(2)]
        block = ctx.enter_context(nc.Block())

        def sequences(eng, body):
            for c in range(4):
                body(Seq(None, c))
            with eng.Fori(2, NB // 2) as i:
                body(Seq(i, 0))
                body(Seq(i, 1))

        @block.gpsimd
        def _(pool):
            pool.sem_inc(begun, 1)
            last_slot = pool.to_reg(E * CAP - 1)

            def gather(c):
                if some(due := computed(pool, c.count(1, -1))):
                    pool.wait_ge(begun, 1)
                    pool.wait_ge(combined, due)
                if some(due := (c + -2).of_parity(16 * K)):
                    pool.wait_ge(gathered[c.par], due)
                nc.gpsimd.tensor_copy(read_at[:, c.par, :], r.slots[:, bass.ds(c.count(K), K)]).then_inc(index_ready, 1)
                due = computed(pool, c.count(1, 1))
                pool.wait_ge(begun, 1)
                pool.wait_ge(index_ready, due)
                for n in range(K):
                    nc.gpsimd.indirect_dma_start(
                        out=eo[:, c.par, n, :], out_offset=None, in_=r.expert_out,
                        in_offset=bass.IndirectOffsetOnAxis(read_at[:, c.par, n:n + 1], 0),
                        bounds_check=last_slot, oob_is_err=False).then_inc(gathered[c.par], 16)
            sequences(pool, gather)

        @block.vector
        def _(dve):
            def tokens(buf, c, t):
                return buf[:, bass.ds(c.count(S, t * D), D)]

            def combine(c):
                dve.wait_ge(gathered[c.par], c.of_parity(16 * K))
                if some(due := (c + -2).of_parity(16)):
                    dve.wait_ge(stored[c.par], due)
                for k in range(TOPK):
                    for t in range(T):
                        n = t * TOPK + k
                        nc.vector.scalar_tensor_tensor(moe[:, t, :], eo[:, c.par, n, :],
                                                       r.gate[:, bass.ds(c.count(K, n), 1)],
                                                       tokens(r.Y, c, t) if k == 0 else moe[:, t, :],
                                                       ALU.mult, ALU.add)
                    dve.drain()
                for t in range(T):
                    last = nc.vector.scalar_tensor_tensor(result[:, c.par, t, :], moe[:, t, :], 0.5,
                                                          tokens(r.X, c, t), ALU.mult, ALU.add)
                last.then_inc(combined, 1)
                dve.drain()
            sequences(dve, combine)

        @block.sync
        def _(sp):
            sp.sem_inc(sp_begun, 1)

            def store(c):
                due = computed(sp, c.count(1, 1))
                sp.wait_ge(sp_begun, 1)
                sp.wait_ge(combined, due)
                if some(due := (c + -2).of_parity(16)):
                    sp.wait_ge(stored[c.par], due)
                sp.dma_start(r.out[bass.ds(c.count(S), S), :].rearrange("(t p) d -> p t d", p=P),
                             result[:, c.par]).then_inc(stored[c.par], 16)
            sequences(sp, store)
            for par in range(2):
                sp.wait_ge(stored[par], 16 * NB // 2)
    give_back(nc, sems)


class Resident:
    pass


def macaron(nc, inp, out):
    r = Resident()
    col = lambda a: a.rearrange("(d a) -> d a", a=1)
    r.x = inp["L0_attn_x"].rearrange("b s d -> (b s) d")
    r.out = out.rearrange("b s d -> (b s) d")
    r.ln1_g, r.ln1_b = col(inp["L0_ffn_ln1_g"]), col(inp["L0_ffn_ln1_b"])
    r.ln2_g, r.ln2_b = col(inp["L0_ffn_ln2_g"]), col(inp["L0_ffn_ln2_b"])
    r.wgate, r.cos, r.sin = inp["L0_ffn_Wgate"], inp["rope_cos"], inp["rope_sin"]
    r.w1 = inp["L0_ffn_W1"].rearrange("e d f -> (e d) f")
    r.w2 = inp["L0_ffn_W2"].rearrange("e f d -> (e f) d")
    r.bias1 = inp["ffn_b1"]
    r.bias2 = inp["L0_ffn_b2"].rearrange("e (d a) -> (e d) a", a=1)
    r.expert_in = nc.dram_tensor("expert_in", [E * CAP, D], F32, kind="Internal").ap()
    r.expert_out = nc.dram_tensor("expert_out", [E * CAP, D], F32, kind="Internal").ap()
    with ExitStack() as ctx:
        def sb(name, shape, dt=F32):
            return ctx.enter_context(nc.sbuf_tensor(name, shape, dt))

        r.X = sb("X", [P, NB * S])
        r.Y = sb("Y", [P, NB * S])
        r.gate = sb("gate", [P, NB * T * TOPK])
        r.slots = sb("slots", [P, NB * T * TOPK], I32)
        r.identf = sb("identf", [P, P])
        r.identb = sb("identb", [P, P], BF16)
        r.above = sb("above", [P, P], BF16)
        r.later = sb("later", [P, P], BF16)
        r.upto = sb("upto", [P, P], BF16)
        r.ones = sb("ones", [P, P], BF16)
        r.iota8 = sb("iota8", [P, E])
        r.minus_half = sb("minus_half", [P, 2])
        iota_i = sb("iota_i", [P, E], I32)
        r.zeros = sb("zeros", [P, 8, D])
        r.stack = sb("stack", [P, 2, 2, T * H, 8, HD], BF16)
        r.V = sb("V", [P, 2, T, H, 32])
        with nc.Block() as block:
            @block.gpsimd
            def _(pool):
                for buf, value in ((r.identf, 0.0), (r.identb, 0.0), (r.above, 0.0), (r.later, 0.0),
                                   (r.upto, 1.0), (r.ones, 1.0),
                                   (r.minus_half, -0.5)):
                    nc.gpsimd.memset(buf[:], value)
                nc.gpsimd.iota(iota_i[:], pattern=[[1, E]], base=0, channel_multiplier=0)
                pool.drain()
                for buf in (r.identf, r.identb):
                    nc.gpsimd.affine_select(out=buf[:], in_=buf[:], compare_op=ALU.not_equal, fill=1.0, base=0,
                                            pattern=[[-1, P]], channel_multiplier=1)
                nc.gpsimd.affine_select(out=r.above[:], in_=r.above[:], compare_op=ALU.is_ge, fill=-BIG, base=0,
                                        pattern=[[-1, P]], channel_multiplier=1)
                nc.gpsimd.affine_select(out=r.later[:], in_=r.later[:], compare_op=ALU.is_ge, fill=-BIG, base=0,
                                        pattern=[[1, P]], channel_multiplier=-1)
                nc.gpsimd.affine_select(out=r.upto[:], in_=r.upto[:], compare_op=ALU.is_ge, fill=0.0, base=0,
                                        pattern=[[1, P]], channel_multiplier=-1)
                nc.gpsimd.tensor_copy(r.iota8[:], iota_i[:])
                pool.drain()

            @block.vector
            def _(dve):
                nc.vector.memset(r.zeros[:], 0.0)
                nc.vector.memset(r.stack[:], 0.0)
                nc.vector.memset(r.V[:], 0.0)
                dve.drain()
                for par in range(2):
                    nc.vector.memset(r.stack[:, par, 1, :, 7, 0:NMAX], 1.0)
                    nc.vector.memset(r.V[:, par, :, :, HD:HD + 1], 1.0)
                dve.drain()

        r.tag, r.loads_x, r.wqkv, r.wout = "f1", True, inp["ffn_Wqkv"], inp["L0_ffn_Wproj"]
        attention_pass(nc, "ffn", r)
        r.tag = "e1"
        expert_pass(nc, r)
        r.tag, r.loads_x, r.wqkv, r.wout = "p", False, inp["attn_Wqkv"], inp["L0_attn_Wo"]
        r.bias = inp["L0_attn_bo"].rearrange("(a d) -> a d", a=1)
        attention_pass(nc, "plain", r)
        r.tag, r.wqkv, r.wout = "f2", inp["ffn_Wqkv"], inp["L0_ffn_Wproj"]
        attention_pass(nc, "ffn", r)
        r.tag = "e2"
        expert_pass(nc, r)
        r.tag = "l"
        last_pass(nc, r)


def laid_out(inputs):
    a = {k: np.asarray(v) for k, v in inputs.items()}
    a["ffn_Wqkv"] = a.pop("L0_ffn_Wqkv").reshape(D, H, 3, HD).transpose(0, 2, 1, 3).reshape(D, 3 * D)
    a["attn_Wqkv"] = np.concatenate([a.pop("L0_attn_Wq"), a.pop("L0_attn_Wk"), a.pop("L0_attn_Wv")], axis=1)
    a["ffn_b1"] = a.pop("L0_ffn_b1").reshape(E, FC, P).transpose(0, 2, 1).reshape(E * P, FC)
    inv_freq = (1.0 / 10000.0 ** (np.arange(0, HD, 2, dtype=np.float32) / HD)).astype(np.float32)
    angle = np.arange(S, dtype=np.float32)[:, None] * inv_freq
    cos, sin = np.cos(angle), np.sin(angle)
    tile = lambda v: v.reshape(T, P, HD).transpose(1, 0, 2).astype(np.float32)
    a["rope_cos"] = tile(np.concatenate([cos, cos], axis=1))
    a["rope_sin"] = tile(np.concatenate([-sin, sin], axis=1))
    return {k: np.ascontiguousarray(v) for k, v in a.items()}


def kernel(**inputs):
    import concourse.bacc as bacc
    from concourse.bass_utils import run_bass_kernel_spmd

    nc = bacc.Bacc("TRN2", target_bir_lowering=False, num_devices=1)
    arrays = laid_out(inputs)
    aps = {k: nc.dram_tensor(f"in_{k}", v.shape, mybir.dt.from_np(v.dtype), kind="ExternalInput").ap()
           for k, v in arrays.items()}
    out = nc.dram_tensor("out", (NB, S, D), F32, kind="ExternalOutput").ap()
    macaron(nc, aps, out)
    result = run_bass_kernel_spmd(nc, [{f"in_{k}": v for k, v in arrays.items()}], core_ids=[0])
    return result.results[0]["out"]
```
